# Optimizing a Trainium2 kernel written in Bass

```python
import numpy as np
import jax
import jax.numpy as jnp

def _softmax(x, axis=-1):
    return jax.nn.softmax(x, axis=axis)
def _gelu(x):
    return jax.nn.gelu(x, approximate=True)
def _silu(x):
    return jax.nn.silu(x)
def _sigmoid(x):
    return jax.nn.sigmoid(x)
def _layernorm(x, axis=-1, eps=1e-5):
    m = jnp.mean(x, axis=axis, keepdims=True)
    v = jnp.var(x, axis=axis, keepdims=True)
    return (x - m) / jnp.sqrt(v + eps)
def _scatter_add(tgt, idx, src, axis=0):
    return tgt.at[idx].add(src)
def _segment_sum(src, seg, n):
    return jax.ops.segment_sum(src, seg, n)

kernel_name = 'mk_conv_seq_d1_conv_nchw256_8d740e'

def setup_inputs(seed: int = 0):
    np.random.seed(seed)
    _w = jnp.asarray
    def _rec_inputs():
        import jax
        import jax.numpy as jnp
        _gk = jax.random.key(seed)
        x = -0.0002091 + 1 * jax.random.normal(jax.random.fold_in(_gk, 1), (32, 256, 56, 56), jnp.float32)
        return x
    x = _rec_inputs()
    def _L0_conv_setup():
        import jax, jax.numpy as jnp
        import numpy as np
        B, C, H, W = (32, 256, 56, 56)
        WS = 7
        NH = 4
        DH = 64
        CMID = 256
        EPS = 1e-05

        def _depthwise(x, w):
            return jax.lax.conv_general_dilated(x, w, window_strides=(1, 1), padding='SAME', feature_group_count=x.shape[1], dimension_numbers=('NCHW', 'OIHW', 'NCHW'))
        key = jax.random.key(seed)
        ks = jax.random.split(key, 12)
        return {'x': jax.random.normal(ks[0], (B, C, H, W), jnp.float32), 'bn_gamma': jnp.ones((C,), jnp.float32), 'bn_beta': jnp.zeros((C,), jnp.float32), 'bn_mean': jnp.zeros((C,), jnp.float32), 'bn_var': jnp.ones((C,), jnp.float32), 'w_qk': jax.random.normal(ks[1], (2 * C, C), jnp.float32) * 0.05, 'w_v': jax.random.normal(ks[2], (CMID, C), jnp.float32) * 0.05, 'w_conv3': jax.random.normal(ks[3], (CMID, 1, 3, 3), jnp.float32) * 0.1, 'w_conv5': jax.random.normal(ks[4], (CMID, 1, 5, 5), jnp.float32) * 0.1, 'w_conv7': jax.random.normal(ks[5], (CMID, 1, 7, 7), jnp.float32) * 0.1, 'attn_w': jax.random.uniform(ks[6], (1, CMID, 1, 1), jnp.float32), 'c3_w': jax.random.uniform(ks[7], (1, CMID, 1, 1), jnp.float32), 'c5_w': jax.random.uniform(ks[8], (1, CMID, 1, 1), jnp.float32), 'c7_w': jax.random.uniform(ks[9], (1, CMID, 1, 1), jnp.float32), 'w_proj': jax.random.normal(ks[10], (C, CMID), jnp.float32) * 0.05}
    _L0_conv_all = _L0_conv_setup()
    _L0_conv_in = {k: v for k, v in _L0_conv_all.items() if k in ('bn_gamma', 'bn_beta', 'bn_mean', 'bn_var', 'w_qk', 'w_v', 'w_conv3', 'w_conv5', 'w_conv7', 'attn_w', 'c3_w', 'c5_w', 'c7_w', 'w_proj', )}
    del _L0_conv_all

    return {
        "x": x,
        "L0_conv_bn_gamma": _L0_conv_in["bn_gamma"],
        "L0_conv_bn_beta": _L0_conv_in["bn_beta"],
        "L0_conv_bn_mean": _L0_conv_in["bn_mean"],
        "L0_conv_bn_var": _L0_conv_in["bn_var"],
        "L0_conv_w_qk": _L0_conv_in["w_qk"],
        "L0_conv_w_v": _L0_conv_in["w_v"],
        "L0_conv_w_conv3": _L0_conv_in["w_conv3"],
        "L0_conv_w_conv5": _L0_conv_in["w_conv5"],
        "L0_conv_w_conv7": _L0_conv_in["w_conv7"],
        "L0_conv_attn_w": _L0_conv_in["attn_w"],
        "L0_conv_c3_w": _L0_conv_in["c3_w"],
        "L0_conv_c5_w": _L0_conv_in["c5_w"],
        "L0_conv_c7_w": _L0_conv_in["c7_w"],
        "L0_conv_w_proj": _L0_conv_in["w_proj"],
    }

def reference(x, L0_conv_bn_gamma, L0_conv_bn_beta, L0_conv_bn_mean, L0_conv_bn_var, L0_conv_w_qk, L0_conv_w_v, L0_conv_w_conv3, L0_conv_w_conv5, L0_conv_w_conv7, L0_conv_attn_w, L0_conv_c3_w, L0_conv_c5_w, L0_conv_c7_w, L0_conv_w_proj):
    import jax
    import jax.numpy as jnp
    def _L0_conv_ref(x, bn_gamma, bn_beta, bn_mean, bn_var, w_qk, w_v, w_conv3, w_conv5, w_conv7, attn_w, c3_w, c5_w, c7_w, w_proj):
        import jax, jax.numpy as jnp
        import numpy as np
        B, C, H, W = (32, 256, 56, 56)
        WS = 7
        NH = 4
        DH = 64
        CMID = 256
        EPS = 1e-05

        def _depthwise(x, w):
            return jax.lax.conv_general_dilated(x, w, window_strides=(1, 1), padding='SAME', feature_group_count=x.shape[1], dimension_numbers=('NCHW', 'OIHW', 'NCHW'))
        shortcut = x
        g = (bn_gamma / jnp.sqrt(bn_var + EPS))[None, :, None, None]
        x = (x - bn_mean[None, :, None, None]) * g + bn_beta[None, :, None, None]
        Bc, Cc, Hc, Wc = x.shape
        n1, n2 = (Hc // WS, Wc // WS)
        xw = x.reshape(Bc, Cc, WS, n1, WS, n2).transpose(0, 3, 5, 1, 2, 4).reshape(Bc * n1 * n2, Cc, WS, WS)
        b = xw.shape[0]
        hw = WS * WS
        qk = jnp.einsum('oc,bchw->bohw', w_qk, xw).reshape(b, 2, NH, DH, hw)
        q = qk[:, 0].transpose(0, 1, 3, 2)
        k = qk[:, 1].transpose(0, 1, 3, 2)
        v = jnp.einsum('oc,bchw->bohw', w_v, xw)
        vh = v.reshape(b, NH, CMID // NH, hw).transpose(0, 1, 3, 2)
        scale = 1.0 / jnp.sqrt(jnp.asarray(DH, x.dtype))
        attn = jax.nn.softmax(jnp.einsum('bnqd,bnkd->bnqk', q, k) * scale, axis=-1)
        x_spa = jnp.einsum('bnqk,bnkd->bnqd', attn, vh).transpose(0, 1, 3, 2).reshape(b, CMID, WS, WS)
        c3 = _depthwise(v, w_conv3)
        c5 = _depthwise(v, w_conv5)
        c7 = _depthwise(v, w_conv7)
        xc = x_spa * attn_w + c3 * c3_w + c5 * c5_w + c7 * c7_w + v
        x = xc.reshape(Bc, n1, n2, CMID, WS, WS).transpose(0, 3, 4, 1, 5, 2).reshape(Bc, CMID, Hc, Wc)
        x = jnp.einsum('oc,bchw->bohw', w_proj, x)
        return shortcut + x

    def _gn(v, G=32, eps=1e-5):
        B_, C_, H_, W_ = v.shape
        g = v.reshape(B_, G, C_ // G, H_, W_)
        m = jnp.mean(g, axis=(2, 3, 4), keepdims=True)
        s = jnp.var(g, axis=(2, 3, 4), keepdims=True)
        return ((g - m) / jnp.sqrt(s + eps)).reshape(v.shape)

    def _ln_c(v, eps=1e-6):
        m = jnp.mean(v, axis=1, keepdims=True)
        s = jnp.var(v, axis=1, keepdims=True)
        return (v - m) / jnp.sqrt(s + eps)

    def _ln_t(v, eps=1e-5):
        m = jnp.mean(v, axis=-1, keepdims=True)
        s = jnp.var(v, axis=-1, keepdims=True)
        return (v - m) / jnp.sqrt(s + eps)

    def _to_tokens(v):
        B_, C_, H_, W_ = v.shape
        return v.reshape(B_, C_, H_ * W_).transpose(0, 2, 1)
    def _from_tokens(t, like):
        B_, C_, H_, W_ = like.shape
        return t.transpose(0, 2, 1).reshape(B_, C_, H_, W_)

    x = _L0_conv_ref(x, L0_conv_bn_gamma, L0_conv_bn_beta, L0_conv_bn_mean, L0_conv_bn_var, L0_conv_w_qk, L0_conv_w_v, L0_conv_w_conv3, L0_conv_w_conv5, L0_conv_w_conv7, L0_conv_attn_w, L0_conv_c3_w, L0_conv_c5_w, L0_conv_c7_w, L0_conv_w_proj)
    return x


_drawn_inputs = setup_inputs


def setup_inputs(seed=0):
    import zlib

    import numpy as np

    out = dict(_drawn_inputs(seed))
    spreads = {'L0_conv_bn_gamma': (1.0, 0.2),
     'L0_conv_bn_beta': (0.0, 0.1),
     'L0_conv_bn_mean': (0.0, 0.1),
     'L0_conv_bn_var': (1.0, 0.2)}
    factors = {}
    for name, (base, spread) in spreads.items():
        noise = np.random.default_rng([zlib.crc32(name.encode()), seed]).standard_normal(out[name].shape)
        drawn = base * np.exp(spread * noise) if base else spread * noise
        out[name] = jnp.asarray(drawn.astype(out[name].dtype))
    for name, factor in factors.items():
        out[name] = (out[name] * factor).astype(out[name].dtype)
    return out
```

```python
from contextlib import ExitStack

import concourse.bass as bass
from concourse import mybir

ALU = mybir.AluOpType
ACT = mybir.ActivationFunctionType
F32 = mybir.dt.float32
AX_X = mybir.AxisListType.X

P = 128
WS = 7
T = WS * WS
DH = 64
EPS = 1e-5


def window_attention_block(nc, x, w_qk_t, w_v_t, w_proj_t, bn, attn_w, conv7, conv5, conv3, conv_w, out):
    B, C, HW = x.shape
    H = W = 56
    N1, N2 = H // WS, W // WS
    KC = C // P
    ROW = N2 * T
    PAD = ROW + DH - T
    PAIRS = N2 // 2
    CP = P
    BANK = 512
    WB = BANK // P
    CSTEPS = CP // 16
    SCALE = float(DH) ** -0.5
    G2 = 13

    ctx = ExitStack()
    with ctx:
        def sb(name, shape):
            return ctx.enter_context(nc.sbuf_tensor(name, shape, F32))

        def sem(name):
            return ctx.enter_context(nc.semaphore(name))

        ps = ctx.enter_context(nc.psum_tensor("ps", [P, 8, BANK], F32))
        QKB, VB, SB, OB = 0, 2, 4, 6

        xb = sb("xb", [P, 2, KC, HW])
        xn = sb("xn", [P, 2, KC, PAD])
        qk = sb("qk", [P, 2, 2, KC, PAD])
        V = sb("V", [P, N1 * N2, CP])
        O = sb("O", [P, 2, N1, ROW])
        taps = sb("taps", [P, CP, DH])
        E = sb("E", [P, 2, N2, T])
        Pn = sb("Pn", [P, PAIRS, KC, 2, DH])
        PT = sb("PT", [P, PAIRS, KC, 2, T])
        xc = sb("xc", [P, 2, 2, ROW])
        mx = sb("mx", [P, 2, N2])
        sm = sb("sm", [P, 2, N2])
        rs = sb("rs", [P, 2, N2])
        wqk = sb("wqk", [P, KC, 2 * C])
        wv = sb("wv", [P, KC, 2, CP])
        wp = sb("wp", [P, 2, C])
        ident = sb("ident", [P, P])
        gate = ctx.enter_context(nc.sbuf_tensor("gate", [P, P], mybir.dt.bfloat16))
        bnp = sb("bnp", [P, 4, KC])
        bna = sb("bna", [P, 5, KC])
        aw = sb("aw", [P, 2])
        cw = sb("cw", [P, 3, KC])
        w7 = sb("w7", [P, KC, WS, WS])
        w5 = sb("w5", [P, KC, 5, 5])
        w3 = sb("w3", [P, KC, 3, 3])
        weff_t = sb("weff_t", [T, 2, KC, DH])
        shift = sb("shift", [T, WS, G2, WS])

        loads = sem("const_loads")
        weights_loaded = sem("weights_loaded")
        inits = sem("inits")
        pool_chain = sem("pool_chain")
        ident_ready = sem("ident_ready")
        chain = sem("dve_chain")
        var_ready = sem("var_ready")
        root_ready = sem("root_ready")
        bn_ready = sem("bn_ready")
        weff_ready = sem("weff_ready")
        wt_done = sem("weff_transposed")
        wt_read = sem("weff_t_ready")
        taps_done = sem("taps_in_psum")
        taps_read = sem("taps_ready")
        x_loaded = sem("x_loaded")
        stored = sem("stored")
        xn_ready = sem("xn_ready")
        qk_done = sem("qk_done")
        qk_read = sem("qk_read")
        v_done = sem("v_done")
        v_read = sem("v_read")
        s_done = sem("s_done")
        max_ready = sem("max_ready")
        s_read = sem("s_read")
        exp_ready = sem("exp_ready")
        sum_ready = sem("sum_ready")
        rec_ready = sem("rec_ready")
        p_ready = sem("p_ready")
        pt_done = sem("pt_done")
        pt_read = sem("pt_read")
        pv_done = sem("pv_done")
        o_read = sem("o_read")
        conv_done = sem("conv_done")
        conv_read_dve = sem("conv_read_dve")
        conv_read_act = sem("conv_read_act")
        ct_done = sem("ct_done")
        xc_ready = sem("xc_ready")
        proj_done = sem("proj_done")
        res_done = sem("res_done")

        R1, R2 = N1, 2 * N1

        x_v = x.rearrange("b (k p) n -> b p k n", p=P)
        out_v = out.rearrange("b (k p) n -> b p k n", p=P)

        def pixels(t, r):
            v = t.rearrange("p (a i b j) -> p i j a b", a=WS, i=N1, b=WS, j=N2)
            return v[:, r]

        block = ctx.enter_context(nc.Block())

        @block.sync
        def _(sp):
            def load(n, buf):
                sp.dma_start(xb[:, buf], x_v[n]).then_inc(x_loaded, 16)

            def store(n, buf):
                sp.dma_start(out_v[n], xb[:, buf]).then_inc(stored, 16)

            for dst, src in ((bnp[:], bn), (w7[:], conv7), (w5[:], conv5), (w3[:], conv3), (cw[:], conv_w),
                             (aw[:], attn_w)):
                sp.dma_start(dst, src).then_inc(loads, 16)
            load(0, 0)
            for dst, src in ((wqk[:, 0], w_qk_t[0]), (wqk[:, 1], w_qk_t[1]), (wv[:], w_v_t), (wp[:], w_proj_t)):
                sp.dma_start(dst, src).then_inc(weights_loaded, 16)
            sp.wait_ge(x_loaded, 16)
            load(1, 1)
            with sp.Fori(0, B - 2) as i:
                sp.wait_ge(res_done, (i + 2) * R2)
                store(i, i % 2)
                sp.wait_ge(stored, (i + 1) * 16)
                sp.wait_ge(x_loaded, (i + 2) * 16)
                load(i + 2, i % 2)
            for i in range(B - 2, B):
                sp.wait_ge(res_done, (i + 2) * R2)
                store(i, i % 2)
            sp.wait_ge(stored, B * 16)

        @block.gpsimd
        def _(pool):
            for t in (xn, qk, Pn, taps, gate):
                nc.gpsimd.memset(t[:], 0.0).then_inc(inits, 1)
            nc.gpsimd.memset(ident[:], 0.0).then_inc(pool_chain, 1)
            nc.gpsimd.memset(shift[:], 0.0).then_inc(pool_chain, 1)
            pool.wait_ge(pool_chain, 2)
            nc.gpsimd.affine_select(out=ident[:], in_=ident[:], compare_op=ALU.not_equal, fill=1.0, base=0,
                                    pattern=[[-1, P]], channel_multiplier=1).then_inc(ident_ready, 1)
            R = WS // 2
            for b_out in range(WS):
                lo, hi = max(0, b_out - R), min(WS, b_out + R + 1)
                mid = shift[:, b_out, R:R + WS, lo:hi]
                m = nc.gpsimd.affine_select(out=mid, in_=mid, compare_op=ALU.not_equal, fill=1.0,
                                            base=-(lo - b_out + R), pattern=[[-WS, WS], [-1, hi - lo]],
                                            channel_multiplier=1)
            m.then_inc(ident_ready, 1)

        @block.tensor
        def _(pe):
            pe.wait_ge(inits, 5)
            pe.wait_ge(ident_ready, 2)
            pe.wait_ge(weff_ready, 1)
            for ob in range(KC):
                m = nc.tensor.transpose(ps[0:T, QKB, ob * P:(ob + 1) * P], w7[:, ob].rearrange("p a b -> p (a b)"),
                                        ident[:])
            m.then_inc(wt_done, 1)
            pe.wait_ge(wt_read, 1)
            for k in range(T):
                a, b = k // WS, k % WS
                if k % WB == 0 and k >= 2 * WB:
                    pe.wait_ge(taps_read, k // WB - 1)
                for e in range(2):
                    m = nc.tensor.matmul(ps[DH * e:DH * e + T, VB + (k // WB) % 2, (k % WB) * P:(k % WB + 1) * P],
                                         shift[:, b, WS - 1 - a:2 * WS - 1 - a].rearrange("p a b -> p (a b)"),
                                         weff_t[:, e].rearrange("p o d -> p (o d)"), start=True, stop=True)
                if k % WB == WB - 1 or k == T - 1:
                    m.then_inc(taps_done, 1)
            pe.wait_ge(taps_read, -(-T // WB))
            pe.wait_ge(weights_loaded, 16 * 4)

            def waits(bank, *counts):
                for s, n in counts:
                    pe.wait_ge(s, n)
                nc.tensor.matmul(ps[:, bank, 0:2], gate[:], gate[:, 0:2], start=True, stop=True)

            def project_qk(i, r):
                pe.wait_ge(xn_ready, i * R1 + r + 1)
                for g in range(4):
                    if r == 0 and g < 2:
                        pe.wait_ge(res_done, (i + 1) * R2)
                    else:
                        pe.wait_ge(qk_read, i * 4 * N1 + 4 * r + g - 1)
                    for kc in range(KC):
                        m = nc.tensor.matmul(ps[:, QKB + g % 2, 0:ROW], wqk[:, kc, g * P:(g + 1) * P],
                                             xn[:, r % 2, kc, 0:ROW], start=(kc == 0), stop=(kc == KC - 1))
                    m.then_inc(qk_done, 1)

            def project_v(i, r):
                for b in range(2):
                    if r == 0:
                        pe.wait_ge(xc_ready, (i + 1) * R2)
                    elif r == 1:
                        pe.wait_ge(v_read, i * R2 + b + 1)
                    else:
                        pe.wait_ge(pt_read, i * R2 + 2 * (r - 2) + b + 1)
                    for j in range(WB * b, WB * (b + 1)):
                        for kc in range(KC):
                            for e in range(2):
                                m = nc.tensor.matmul(
                                    ps[DH * e:DH * (e + 1), VB + b, (j % WB) * P:(j % WB + 1) * P],
                                    xn[:, r % 2, kc, j * T:j * T + DH], wv[:, kc, e],
                                    start=(kc == 0), stop=(kc == KC - 1))
                    m.then_inc(v_done, 1)

            def scores(i, r):
                waits(SB, (qk_read, i * 4 * N1 + 4 * (r + 1)), (s_read, i * R1 + r) if r else (xc_ready, (i + 1) * R2))
                for p in range(PAIRS):
                    for ob in range(KC):
                        for w in range(2):
                            for e in range(2):
                                t = (2 * p + w) * T
                                s = (p * KC + ob) * T
                                m = nc.tensor.matmul(ps[DH * w:DH * (w + 1), SB + e, s:s + T],
                                                     qk[DH * e:DH * (e + 1), r % 2, 0, ob, t:t + DH],
                                                     qk[DH * e:DH * (e + 1), r % 2, 1, ob, t:t + T],
                                                     start=True, stop=True)
                m.then_inc(s_done, 1)

            def transpose_p(i, r):
                pe.wait_ge(p_ready, i * R1 + r + 1)
                for b in range(2):
                    pe.wait_ge(v_read, i * R2 + 2 * min(r + 1, N1 - 1) + b + 1)
                    for p in range(2 * b, 2 * b + 2):
                        for ob in range(KC):
                            s = ((p % 2) * KC + ob) * P
                            m = nc.tensor.transpose(ps[:, VB + b, s:s + P],
                                                    Pn[:, p, ob].rearrange("p e k -> p (e k)"), ident[:])
                    m.then_inc(pt_done, 1)

            def attend(i, r):
                waits(OB, (pt_read, i * R2 + 2 * (r + 1)), (o_read, i * R2 + 2 * r) if r else (res_done, (i + 1) * R2))
                for j in range(N2):
                    for ob in range(KC):
                        for e in range(2):
                            m = nc.tensor.matmul(ps[DH * ob:DH * (ob + 1), OB + e, j * T:(j + 1) * T],
                                                 V[DH * e:DH * e + T, r * N2 + j, ob * DH:(ob + 1) * DH],
                                                 PT[DH * e:DH * e + T, j // 2, ob, j % 2],
                                                 start=True, stop=True)
                m.then_inc(pv_done, 1)

            def convolve(i, s):
                first = QKB if s % 2 == 0 else SB
                if s == 0:
                    waits(QKB, (v_read, (i + 1) * R2), (qk_read, (i + 1) * 4 * N1))
                elif s == 1:
                    waits(SB, (s_read, (i + 1) * R1))
                else:
                    waits(first, (conv_read_dve, i * CSTEPS + s - 1), (conv_read_act, i * CSTEPS + s - 1))
                for swap in range(2):
                    for n in range(8):
                        for e in range(2):
                            b = e ^ swap
                            cp = 16 * s + 8 * b + n
                            m = nc.tensor.matmul(ps[DH * e:DH * (e + 1), first + b, n * N1 * N2:(n + 1) * N1 * N2],
                                                 taps[DH * e:DH * e + T, cp, :], V[DH * e:DH * e + T, :, cp],
                                                 start=True, stop=True)
                m.then_inc(conv_done, 1)

            def transpose_conv(i, r):
                if r == 0:
                    pe.wait_ge(conv_read_dve, (i + 1) * CSTEPS)
                    pe.wait_ge(conv_read_act, (i + 1) * CSTEPS)
                    pe.wait_ge(pt_read, (i + 1) * R2)
                elif r >= 2:
                    pe.wait_ge(xc_ready, (i + 1) * R2 + 2 * (r - 1))
                first = VB if r % 2 == 0 else SB
                for j in range(N2):
                    m = nc.tensor.transpose(ps[:, first + j // WB, (j % WB) * P:(j % WB + 1) * P],
                                            V[:, r * N2 + j], ident[:])
                    if j % WB == WB - 1:
                        m.then_inc(ct_done, 1)

            def project_out(i, r):
                pe.wait_ge(xc_ready, (i + 1) * R2 + 2 * (r + 1))
                if r == 1:
                    pe.wait_ge(o_read, (i + 1) * R2)
                elif r >= 2:
                    pe.wait_ge(res_done, (i + 1) * R2 + 2 * (r - 1))
                first = QKB if r % 2 == 0 else OB
                for ob in range(KC):
                    for e in range(2):
                        m = nc.tensor.matmul(ps[:, first + ob, 0:ROW], wp[:, e, ob * P:(ob + 1) * P],
                                             xc[:, r % 2, e], start=(e == 0), stop=(e == 1))
                    m.then_inc(proj_done, 1)

            with pe.Fori(0, B) as i:
                for r in range(N1):
                    project_qk(i, r)
                    project_v(i, r)
                    if r:
                        transpose_p(i, r - 1)
                    scores(i, r)
                    if r:
                        attend(i, r - 1)
                convolve(i, 0)
                transpose_p(i, N1 - 1)
                convolve(i, 1)
                attend(i, N1 - 1)
                for s in range(2, CSTEPS):
                    convolve(i, s)
                transpose_conv(i, 0)
                for r in range(N1):
                    if r + 1 < N1:
                        transpose_conv(i, r + 1)
                    project_out(i, r)

        @block.scalar
        def _(act):
            act.wait_ge(var_ready, 1)
            nc.scalar.activation(bna[:, 1], bna[:, 0], ACT.Sqrt).then_inc(root_ready, 1)
            act.wait_ge(bn_ready, 1)
            act.wait_ge(inits, 5)

            def normalise(i, r):
                if r == 0:
                    act.wait_ge(x_loaded, (i + 1) * 16)
                elif r >= 2:
                    act.wait_ge(v_done, i * R2 + 2 * (r - 1))
                for kc in range(KC):
                    m = nc.scalar.activation(
                        xn[:, r % 2, kc, 0:ROW].rearrange("p (j a b) -> p j a b", a=WS, b=WS),
                        pixels(xb[:, i % 2, kc], r), ACT.Identity,
                        bias=bna[:, 3, kc:kc + 1], scale=bna[:, 2, kc:kc + 1])
                m.then_inc(xn_ready, 1)

            def read_qk(i, r):
                if r >= 2:
                    act.wait_ge(s_done, i * R1 + r - 1)
                for g in range(4):
                    act.wait_ge(qk_done, i * 4 * N1 + 4 * r + g + 1)
                    nc.scalar.copy(qk[:, r % 2, g // 2, g % 2, 0:ROW], ps[:, QKB + g % 2, 0:ROW]).then_inc(qk_read, 1)

            def exponentials(i, r):
                act.wait_ge(s_read, i * R1 + r + 1)
                nc.scalar.activation(E[:], E[:], ACT.Exp, scale=SCALE).then_inc(exp_ready, 1)

            def read_o(i, r):
                act.wait_ge(pv_done, i * R1 + r + 1)
                for e in range(2):
                    nc.scalar.mul(O[:, e, r], ps[:, OB + e, 0:ROW], aw[:, e:e + 1]).then_inc(o_read, 1)

            def read_conv(i, s):
                if s == 0:
                    act.wait_ge(pv_done, (i + 1) * R1)
                act.wait_ge(conv_done, i * CSTEPS + s + 1)
                first = QKB if s % 2 == 0 else SB
                nc.scalar.copy(V[:, :, 16 * s + 8:16 * s + 16],
                               ps[:, first + 1].rearrange("p (n w) -> p w n", n=8)).then_inc(conv_read_act, 1)

            with act.Fori(0, B) as i:
                normalise(i, 0)
                for r in range(N1):
                    read_qk(i, r)
                    if r + 1 < N1:
                        normalise(i, r + 1)
                    if r:
                        read_o(i, r - 1)
                    exponentials(i, r)
                read_o(i, N1 - 1)
                for s in range(CSTEPS):
                    read_conv(i, s)

        @block.vector
        def _(dve):
            dve.wait_ge(loads, 16 * 6)
            steps = [0]

            def then(ins):
                steps[0] += 1
                ins.then_inc(chain, 1)
                dve.wait_ge(chain, steps[0])

            gamma, beta, mean, var = (bnp[:, n] for n in range(4))
            vare, root, scale, bias, tmp = (bna[:, n] for n in range(5))
            nc.vector.tensor_scalar(vare, var, EPS, None, ALU.add).then_inc(var_ready, 1)
            dve.wait_ge(root_ready, 1)
            then(nc.vector.reciprocal(tmp, root))
            then(nc.vector.tensor_tensor(tmp, tmp, vare, ALU.mult))
            then(nc.vector.tensor_tensor(tmp, tmp, root, ALU.add))
            then(nc.vector.tensor_scalar(root, tmp, 0.5, None, ALU.mult))
            then(nc.vector.reciprocal(tmp, root))
            then(nc.vector.tensor_tensor(scale, gamma, tmp, ALU.mult))
            then(nc.vector.tensor_tensor(tmp, mean, scale, ALU.mult))
            nc.vector.tensor_tensor(bias, beta, tmp, ALU.subtract).then_inc(bn_ready, 1)
            for ob in range(KC):
                then(nc.vector.tensor_scalar(w7[:, ob], w7[:, ob], cw[:, 0, ob:ob + 1], None, ALU.mult))
                for n, (w, m) in enumerate(((w5, 5), (w3, 3))):
                    o = (WS - m) // 2
                    mid = w7[:, ob, o:o + m, o:o + m]
                    then(nc.vector.scalar_tensor_tensor(out=mid, in0=w[:, ob], scalar=cw[:, n + 1, ob:ob + 1],
                                                        in1=mid, op0=ALU.mult, op1=ALU.add))
                one = w7[:, ob, WS // 2, WS // 2:WS // 2 + 1]
                m = nc.vector.tensor_scalar(one, one, 1.0, None, ALU.add)
                if ob + 1 < KC:
                    then(m)
            m.then_inc(weff_ready, 1)
            dve.wait_ge(wt_done, 1)
            nc.vector.tensor_copy(weff_t[:].rearrange("p e o d -> p o e d"),
                                  ps[0:T, QKB, 0:C].rearrange("p (o e d) -> p o e d", o=KC, e=2)).then_inc(wt_read, 1)
            dve.wait_ge(inits, 5)
            for g in range(-(-T // WB)):
                dve.wait_ge(taps_done, g + 1)
                n = min(WB, T - g * WB)
                for e in range(2):
                    m = nc.vector.tensor_copy(
                        taps[DH * e:DH * e + T, :, g * WB:g * WB + n],
                        ps[DH * e:DH * e + T, VB + g % 2, 0:n * P].rearrange("p (k c) -> p c k", k=n))
                m.then_inc(taps_read, 1)
            nc.vector.memset(mx[:], 0.0).then_inc(res_done, R2)
            nc.vector.memset(sm[:], 0.0).then_inc(xc_ready, R2)

            def read_v(i, r):
                for b in range(2):
                    dve.wait_ge(v_done, i * R2 + 2 * r + b + 1)
                    nc.vector.tensor_copy(V[:, r * N2 + WB * b:r * N2 + WB * (b + 1)].rearrange("p w c -> p (w c)"),
                                          ps[:, VB + b]).then_inc(v_read, 1)

            S = ps[:, SB:SB + 2, 0:ROW].rearrange("p e (g k) -> p e g k", k=T)

            def softmax_shift(i, r):
                dve.wait_ge(s_done, i * R1 + r + 1)
                nc.vector.tensor_reduce(mx[:], S, AX_X, ALU.max).then_inc(max_ready, 1)
                dve.wait_ge(max_ready, i * R1 + r + 1)
                nc.vector.tensor_tensor(E[:], S, mx[:].unsqueeze(3).broadcast_to([P, 2, N2, T]),
                                        ALU.subtract).then_inc(s_read, 1)

            def softmax_norm(i, r):
                dve.wait_ge(exp_ready, i * R1 + r + 1)
                nc.vector.tensor_reduce(sm[:], E[:], AX_X, ALU.add).then_inc(sum_ready, 1)
                dve.wait_ge(sum_ready, i * R1 + r + 1)
                nc.vector.reciprocal(rs[:], sm[:]).then_inc(rec_ready, 1)
                dve.wait_ge(rec_ready, i * R1 + r + 1)
                nc.vector.tensor_tensor(Pn[:, :, :, :, 0:T].rearrange("p r o e k -> p e (r o) k"), E[:],
                                        rs[:].unsqueeze(3).broadcast_to([P, 2, N2, T]), ALU.mult).then_inc(p_ready, 1)

            def read_pt(i, r):
                for b in range(2):
                    dve.wait_ge(pt_done, i * R2 + 2 * r + b + 1)
                    nc.vector.tensor_copy(
                        PT[:, 2 * b:2 * b + 2].rearrange("p r o w q -> p (r o) w q"),
                        ps[:, VB + b].rearrange("p (g w q) -> p g w q", g=2 * KC, w=2)[:, :, :, 0:T]).then_inc(pt_read, 1)

            def read_conv(i, s):
                if s == 0:
                    dve.wait_ge(pv_done, (i + 1) * R1)
                dve.wait_ge(conv_done, i * CSTEPS + s + 1)
                first = QKB if s % 2 == 0 else SB
                nc.vector.tensor_copy(V[:, :, 16 * s:16 * s + 8],
                                      ps[:, first].rearrange("p (n w) -> p w n", n=8)).then_inc(conv_read_dve, 1)

            def combine(i, r):
                if r == 0:
                    dve.wait_ge(o_read, (i + 1) * R2)
                first = VB if r % 2 == 0 else SB
                for b in range(2):
                    dve.wait_ge(ct_done, i * R2 + 2 * r + b + 1)
                    t = slice(b * WB * T, (b + 1) * WB * T)
                    nc.vector.tensor_tensor(
                        xc[:, r % 2, :, t].rearrange("p e (j q) -> p e j q", q=T),
                        ps[:, first + b].rearrange("p (j e q) -> p e j q", j=WB, e=2)[:, :, :, 0:T],
                        O[:, :, r, t].rearrange("p e (j q) -> p e j q", q=T), ALU.add).then_inc(xc_ready, 1)

            def residual(i, r):
                first = QKB if r % 2 == 0 else OB
                for ob in range(KC):
                    dve.wait_ge(proj_done, i * R2 + 2 * r + ob + 1)
                    px = pixels(xb[:, i % 2, ob], r)
                    nc.vector.tensor_tensor(px, ps[:, first + ob, 0:ROW].rearrange("p (j a b) -> p j a b", a=WS, b=WS),
                                            px, ALU.add).then_inc(res_done, 1)

            with dve.Fori(0, B) as i:
                for r in range(N1):
                    if r:
                        softmax_norm(i, r - 1)
                    read_v(i, r)
                    if r:
                        read_pt(i, r - 1)
                    softmax_shift(i, r)
                softmax_norm(i, N1 - 1)
                read_pt(i, N1 - 1)
                for s in range(CSTEPS):
                    read_conv(i, s)
                combine(i, 0)
                for r in range(N1):
                    if r + 1 < N1:
                        combine(i, r + 1)
                    residual(i, r)


def kernel(x, L0_conv_bn_gamma, L0_conv_bn_beta, L0_conv_bn_mean, L0_conv_bn_var, L0_conv_w_qk, L0_conv_w_v,
           L0_conv_w_conv3, L0_conv_w_conv5, L0_conv_w_conv7, L0_conv_attn_w, L0_conv_c3_w, L0_conv_c5_w,
           L0_conv_c7_w, L0_conv_w_proj):
    import concourse.bacc as bacc
    import numpy as np
    from concourse.bass_utils import run_bass_kernel_spmd

    x = np.asarray(x)
    B, C, H, W = x.shape
    KC = C // P

    def halves(a):
        a = np.asarray(a)
        return np.ascontiguousarray(np.moveaxis(a.reshape(KC, P, *a.shape[1:]), 0, 1))

    w_qk, w_v, w_proj = (np.asarray(a) for a in (L0_conv_w_qk, L0_conv_w_v, L0_conv_w_proj))
    arrays = {
        "x": x.reshape(B, C, H * W),
        "w_qk_t": np.ascontiguousarray(w_qk.T).reshape(KC, P, 2 * C),
        "w_v_t": np.ascontiguousarray(w_v.T.reshape(KC, P, KC, 2, DH).transpose(1, 0, 3, 2, 4)).reshape(P, KC, 2, P),
        "w_proj_t": np.ascontiguousarray(w_proj.T.reshape(KC, 2, DH, C).transpose(0, 2, 1, 3)).reshape(P, 2, C),
        "bn": np.ascontiguousarray(np.stack([halves(a) for a in (L0_conv_bn_gamma, L0_conv_bn_beta, L0_conv_bn_mean,
                                                                 L0_conv_bn_var)], axis=1)),
        "attn_w": np.ascontiguousarray(np.asarray(L0_conv_attn_w).reshape(KC, 2, DH).transpose(0, 2, 1)).reshape(P, 2),
        "conv7": halves(np.asarray(L0_conv_w_conv7)[:, 0]),
        "conv5": halves(np.asarray(L0_conv_w_conv5)[:, 0]),
        "conv3": halves(np.asarray(L0_conv_w_conv3)[:, 0]),
        "conv_w": np.ascontiguousarray(np.stack([halves(np.asarray(a).reshape(C)) for a in
                                                 (L0_conv_c7_w, L0_conv_c5_w, L0_conv_c3_w)], axis=1)),
    }
    nc = bacc.Bacc("TRN2", target_bir_lowering=False, num_devices=1)
    args = [nc.dram_tensor(f"in_{n}", a.shape, mybir.dt.from_np(a.dtype), kind="ExternalInput").ap()
            for n, a in arrays.items()]
    out = nc.dram_tensor("out_x", (B, C, H * W), F32, kind="ExternalOutput").ap()
    window_attention_block(nc, *args, out)
    r = run_bass_kernel_spmd(nc, [{f"in_{n}": a for n, a in arrays.items()}], core_ids=[0])
    return r.results[0]["out_x"].reshape(B, C, H, W)
```

```python
from contextlib import ExitStack

import concourse.bass as bass
from concourse import mybir

ALU = mybir.AluOpType
ACT = mybir.ActivationFunctionType
F32 = mybir.dt.float32
F16 = mybir.dt.float16
AX_X = mybir.AxisListType.X

P = 128
WS = 7
T = WS * WS
DH = 64
EPS = 1e-5


def window_attention_block(nc, x, w_qk_t, w_v_t, w_proj_t, bn, attn_w, conv7, conv5, conv3, conv_w, out):
    B, C, HW = x.shape
    H = W = 56
    N1, N2 = H // WS, W // WS
    KC = C // P
    ROW = N2 * T
    PAD = ROW + DH - T
    PAIRS = N2 // 2
    CP = P
    BANK = 512
    WB = BANK // P
    NW = N1 * N2
    CB = BANK // NW
    CSTEPS = CP // (2 * CB)
    SCALE = float(DH) ** -0.5
    G2 = 13
    UP = 64.0
    UP_OUT = 8.0
    PASSES = ((0, 0), (0, 1), (1, 0))
    NP = len(PASSES)

    ctx = ExitStack()
    with ctx:
        def sb(name, shape, dt=F32):
            return ctx.enter_context(nc.sbuf_tensor(name, shape, dt))

        def sem(name):
            return ctx.enter_context(nc.semaphore(name))

        ps = ctx.enter_context(nc.psum_tensor("ps", [P, 8, BANK], F32))
        QKB, VB, SB, OB = 0, 2, 4, 6

        CONVB = (SB, QKB, VB, OB)

        xb = sb("xb", [P, 2, KC, HW])
        xf = sb("xf", [P, KC, ROW])
        xn = sb("xn", [P, 2, 2, KC, PAD], F16)
        qk = sb("qk", [P, 2, 2, KC, PAD], F16)
        V = sb("V", [P, 2, NW, CP], F16)
        O = sb("O", [P, 2, N1, ROW])
        taps = sb("taps", [P, 2, CP, P], F16)
        Pn = sb("Pn", [P, PAIRS, KC, 2, DH])
        xc = sb("xc", [P, 2, 2, 2, ROW], F16)
        mx = sb("mx", [P, 2, N2])
        sm = sb("sm", [P, 2, N2])
        rs = sb("rs", [P, 2, N2])
        wqk = sb("wqk", [P, 2, KC, 2 * C], F16)
        wv = sb("wv", [P, 2, KC, 2, CP], F16)
        wp = sb("wp", [P, 2, 2, C], F16)
        ident = sb("ident", [P, P])
        eighth = sb("eighth", [P, P], F16)
        bnp = sb("bnp", [P, 4, KC])
        bna = sb("bna", [P, 5, KC])
        aw = sb("aw", [P, 2])
        cw = sb("cw", [P, 3, KC])
        pt_xcs = sb("pt_xcs", [P, 2 * ROW])
        PT = pt_xcs[:].bitcast(F16).rearrange("p (u r o w q) -> p u r o w q", u=2, r=PAIRS, o=KC, w=2)
        xcs = pt_xcs[:].rearrange("p (e t) -> p e t", e=2)
        stage, used = O[:].rearrange("p e r t -> p (e r t)"), [0]

        def staged(n, parts=P):
            used[0] += n
            return stage[0:parts, used[0] - n:used[0]]

        w_in = staged(KC * 2 * C + KC * 2 * CP + 2 * C)
        w7 = staged(KC * T).rearrange("p (o a b) -> p o a b", a=WS, b=WS)
        w5 = staged(KC * 25).rearrange("p (o a b) -> p o a b", a=5, b=5)
        w3 = staged(KC * 9).rearrange("p (o a b) -> p o a b", a=3, b=3)
        weff_t = staged(C, T).rearrange("p (e o d) -> p e o d", e=2, o=KC)
        shift = staged(WS * G2 * WS, T).rearrange("p (c a b) -> p c a b", a=G2, b=WS)
        NQ, NV = KC * 2 * C, KC * 2 * CP

        loads = sem("const_loads")
        weights_loaded = sem("weights_loaded")
        inits = sem("inits")
        pool_chain = sem("pool_chain")
        ident_ready = sem("ident_ready")
        chain = sem("dve_chain")
        var_ready = sem("var_ready")
        root_ready = sem("root_ready")
        bn_ready = sem("bn_ready")
        weff_ready = sem("weff_ready")
        wt_done = sem("weff_transposed")
        wt_read = sem("weff_t_ready")
        taps_done = sem("taps_in_psum")
        taps_hi = sem("taps_hi")
        taps_lo = sem("taps_lo")
        weights_hi = sem("weights_hi")
        weights_lo = sem("weights_lo")
        x_loaded = sem("x_loaded")
        stored = sem("stored")
        xf_ready = sem("xf_ready")
        xn_hi = sem("xn_hi")
        xn_lo = sem("xn_lo")
        qk_done = sem("qk_done")
        qk_hi = sem("qk_hi")
        qk_lo = sem("qk_lo")
        v_done = sem("v_done")
        v_hi = sem("v_hi")
        v_lo = sem("v_lo")
        s_done = sem("s_done")
        max_ready = sem("max_ready")
        s_read = sem("s_read")
        exp_ready = sem("exp_ready")
        sum_ready = sem("sum_ready")
        rec_ready = sem("rec_ready")
        p_ready = sem("p_ready")
        pt_done = sem("pt_done")
        pt_hi = sem("pt_hi")
        pt_lo = sem("pt_lo")
        pv_done = sem("pv_done")
        o_read = sem("o_read")
        conv_done = sem("conv_done")
        conv_hi = sem("conv_hi")
        conv_lo = sem("conv_lo")
        ct_done = sem("ct_done")
        xcs_ready = sem("xcs_ready")
        xc_hi = sem("xc_hi")
        xc_lo = sem("xc_lo")
        proj_done = sem("proj_done")
        res_done = sem("res_done")

        R1, R2, R4 = N1, 2 * N1, 4 * N1
        C2 = 2 * CSTEPS

        x_v = x.rearrange("b (k p) n -> b p k n", p=P)
        out_v = out.rearrange("b (k p) n -> b p k n", p=P)

        def pixels(t, r):
            v = t.rearrange("p (a i b j) -> p i j a b", a=WS, i=N1, b=WS, j=N2)
            return v[:, r]

        Pw = Pn[:, :, :, :, 0:T].rearrange("p r o e k -> p e (r o) k")
        S = ps[:, SB:SB + 2, 0:ROW].rearrange("p e (g k) -> p e g k", k=T)
        TAPS_ZERO = 2

        block = ctx.enter_context(nc.Block())

        @block.sync
        def _(sp):
            def load(n, buf):
                sp.dma_start(xb[:, buf], x_v[n]).then_inc(x_loaded, 16)

            def store(n, buf):
                sp.dma_start(out_v[n], xb[:, buf]).then_inc(stored, 16)

            for dst, src in ((bnp[:], bn), (w7, conv7), (w5, conv5), (w3, conv3), (cw[:], conv_w),
                             (aw[:], attn_w)):
                sp.dma_start(dst, src).then_inc(loads, 16)
            load(0, 0)
            for dst, src in ((w_in[:, 0:NQ], w_qk_t), (w_in[:, NQ:NQ + NV], w_v_t), (w_in[:, NQ + NV:], w_proj_t)):
                sp.dma_start(dst, src).then_inc(weights_loaded, 16)
            sp.wait_ge(x_loaded, 16)
            load(1, 1)
            with sp.Fori(0, B - 2) as i:
                sp.wait_ge(res_done, (i + 2) * R2)
                store(i, i % 2)
                sp.wait_ge(stored, (i + 1) * 16)
                sp.wait_ge(x_loaded, (i + 2) * 16)
                load(i + 2, i % 2)
            for i in range(B - 2, B):
                sp.wait_ge(res_done, (i + 2) * R2)
                store(i, i % 2)
                if i == B - 2:
                    sp.wait_ge(x_loaded, B * 16)
                    sp.sem_inc(x_loaded, 16)
            sp.wait_ge(stored, B * 16)

        @block.gpsimd
        def _(pool):
            nc.gpsimd.memset(ident[:], 0.0).then_inc(pool_chain, 1)
            nc.gpsimd.memset(shift, 0.0).then_inc(pool_chain, 1)
            pool.wait_ge(pool_chain, 2)
            nc.gpsimd.affine_select(out=ident[:], in_=ident[:], compare_op=ALU.not_equal, fill=1.0, base=0,
                                    pattern=[[-1, P]], channel_multiplier=1).then_inc(ident_ready, 1)
            R = WS // 2
            for b_out in range(WS):
                lo, hi = max(0, b_out - R), min(WS, b_out + R + 1)
                mid = shift[:, b_out, R:R + WS, lo:hi]
                m = nc.gpsimd.affine_select(out=mid, in_=mid, compare_op=ALU.not_equal, fill=1.0,
                                            base=-(lo - b_out + R), pattern=[[-WS, WS], [-1, hi - lo]],
                                            channel_multiplier=1)
            m.then_inc(ident_ready, 1)
            for t in (xn, qk, Pn):
                nc.gpsimd.memset(t[:], 0.0).then_inc(inits, 1)

            def xn_low(i, r):
                if r >= 2:
                    pool.wait_ge(v_done, i * R2 + 2 * (r - 1))
                pool.wait_ge(xn_hi, i * R1 + r + 1)
                nc.gpsimd.tensor_tensor(xn[:, 1, r % 2, :, 0:ROW], xf[:], xn[:, 0, r % 2, :, 0:ROW],
                                        ALU.subtract).then_inc(xn_lo, 1)

            def xc_low(i, r):
                for b in range(2):
                    t = slice(b * WB * T, (b + 1) * WB * T)
                    pool.wait_ge(xc_hi, i * R2 + 2 * r + b + 1)
                    nc.gpsimd.tensor_tensor(xc[:, 1, r % 2, :, t], xcs[:, :, t], xc[:, 0, r % 2, :, t],
                                            ALU.subtract).then_inc(xc_lo, 1)

            nc.gpsimd.memset(mx[:], 0.0).then_inc(xc_lo, R2)
            xn_low(0, 0)
            xn_low(0, 1)
            with pool.Fori(0, B) as i:
                for r in range(2, N1 + 1):
                    xn_low(i, r)
                for r in range(N1):
                    xc_low(i, r)
                    if r == 3:
                        xn_low(i, N1 + 1)

        @block.tensor
        def _(pe):
            pe.wait_ge(ident_ready, 2)
            pe.wait_ge(weff_ready, 1)
            for ob in range(KC):
                m = nc.tensor.transpose(ps[0:T, QKB, ob * P:(ob + 1) * P], w7[:, ob].rearrange("p a b -> p (a b)"),
                                        ident[:])
            m.then_inc(wt_done, 1)
            pe.wait_ge(wt_read, 1)
            for k in range(T):
                a, b = k // WS, k % WS
                if k % WB == 0 and k >= 2 * WB:
                    pe.wait_ge(taps_lo, k // WB - 1)
                for e in range(2):
                    m = nc.tensor.matmul(ps[DH * e:DH * e + T, VB + (k // WB) % 2, (k % WB) * P:(k % WB + 1) * P],
                                         shift[:, b, WS - 1 - a:2 * WS - 1 - a].rearrange("p a b -> p (a b)"),
                                         weff_t[:, e].rearrange("p o d -> p (o d)"), start=True, stop=True)
                if k % WB == WB - 1 or k == T - 1:
                    m.then_inc(taps_done, 1)
            pe.wait_ge(taps_lo, -(-T // WB))
            pe.wait_ge(weights_lo, 3)
            pe.wait_ge(inits, 4)

            def waits(bank, *counts):
                for s, n in counts:
                    pe.wait_ge(s, n)
                nc.tensor.matmul(ps[:, bank, 0:2], eighth[:], eighth[:, 0:2], start=True, stop=True)

            def project_qk(i, r):
                pe.wait_ge(xn_lo, i * R1 + r + 1)
                for g in range(4):
                    if r or g >= 2:
                        pe.wait_ge(qk_lo, i * R4 + 4 * r + g - 1)
                    for n, (u, v) in enumerate(PASSES):
                        for kc in range(KC):
                            m = nc.tensor.matmul(ps[:, QKB + g % 2, 0:ROW], wqk[:, u, kc, g * P:(g + 1) * P],
                                                 xn[:, v, r % 2, kc, 0:ROW], start=(n == 0 and kc == 0),
                                                 stop=(n == NP - 1 and kc == KC - 1))
                    m.then_inc(qk_done, 1)
                    if r >= 2:
                        for part in ((0,), (1,), (2, 3), ())[g]:
                            attend(i, r - 2, part)
                    if r and g == 2:
                        transpose_p(i, r - 1)

            def project_v(i, r):
                for b in range(2):
                    if r:
                        pe.wait_ge(pt_lo, i * R2 + 2 * (r - 1) + b + 1)
                    for j in range(WB * b, WB * (b + 1)):
                        for n, (u, v) in enumerate(PASSES):
                            for kc in range(KC):
                                for e in range(2):
                                    m = nc.tensor.matmul(
                                        ps[DH * e:DH * (e + 1), VB + b, (j % WB) * P:(j % WB + 1) * P],
                                        xn[:, u, r % 2, kc, j * T:j * T + DH], wv[:, v, kc, e],
                                        start=(n == 0 and kc == 0), stop=(n == NP - 1 and kc == KC - 1))
                        if j % WB == WB - 1:
                            m.then_inc(v_done, 1)
                        if j == 2 and r < N1:
                            scores_start(i, r)
                        if j >= 2 and r < N1:
                            for g in range(*SCORE_TURNS[j - 2]):
                                scores(i, r, g)

            SCORE_TURNS = ((0, 4), (4, 8), (8, 11), (11, 14), (14, 16), (16, 16))

            def scores_start(i, r):
                waits(SB, (qk_lo, i * R4 + 4 * (r + 1)), *([(s_read, i * R1 + r)] if r else []))

            def scores(i, r, g):
                p, ob, w = g // 4, g // 2 % 2, g % 2
                t = (2 * p + w) * T
                s = (p * KC + ob) * T
                for n, (u, v) in enumerate(PASSES):
                    for e in range(2):
                        m = nc.tensor.matmul(ps[DH * w:DH * (w + 1), SB + e, s:s + T],
                                             qk[DH * e:DH * (e + 1), u, 0, ob, t:t + DH],
                                             qk[DH * e:DH * (e + 1), v, 1, ob, t:t + T],
                                             start=(n == 0), stop=(n == NP - 1))
                if g == 2 * N2 - 1:
                    m.then_inc(s_done, 1)

            def transpose_p(i, r):
                pe.wait_ge(p_ready, i * R1 + r + 1)
                for b in range(2):
                    if r:
                        pe.wait_ge(v_lo, i * R2 + 2 * r + b + 1)
                    else:
                        pe.wait_ge(res_done, (i + 1) * R2)
                    for p in range(2 * b, 2 * b + 2):
                        for ob in range(KC):
                            s = ((p % 2) * KC + ob) * P
                            m = nc.tensor.transpose(ps[:, VB + b, s:s + P],
                                                    Pn[:, p, ob].rearrange("p e k -> p (e k)"), ident[:])
                    m.then_inc(pt_done, 1)

            def attend(i, r, part):
                if part == 0:
                    waits(OB, (pt_lo, i * R2 + 2 * (r + 1)), *([(o_read, i * R2 + 2 * r)] if r else []))
                for j in range(2 * part, 2 * part + 2):
                    for n, (u, v) in enumerate(PASSES):
                        for ob in range(KC):
                            for e in range(2):
                                m = nc.tensor.matmul(ps[DH * ob:DH * (ob + 1), OB + e, j * T:(j + 1) * T],
                                                     V[DH * e:DH * e + T, u, r * N2 + j, ob * DH:(ob + 1) * DH],
                                                     PT[DH * e:DH * e + T, v, j // 2, ob, j % 2],
                                                     start=(n == 0), stop=(n == NP - 1))
                if part == 3:
                    m.then_inc(pv_done, 1)

            def convolve_bank(i, s, b):
                first = CONVB[s % 4]
                if s == 0 and b == 0:
                    pe.wait_ge(v_lo, (i + 1) * R2)
                if s == 0:
                    pe.wait_ge(s_read, (i + 1) * R1)
                elif s == 1:
                    pe.wait_ge(qk_lo, (i + 1) * R4 + 4)
                elif s == 2:
                    pe.wait_ge(pt_lo, (i + 1) * R2)
                elif s == 3:
                    pe.wait_ge(o_read, (i + 1) * R2)
                else:
                    pe.wait_ge(conv_lo, i * C2 + 2 * (s - 4) + b + 1)
                for n8 in range(CB):
                    cp = (2 * s + b) * CB + n8
                    for n, (u, v) in enumerate(PASSES):
                        m = nc.tensor.matmul(ps[:, first + b, n8 * NW:(n8 + 1) * NW], taps[:, u, cp],
                                             V[:, v, :, cp], start=(n == 0), stop=(n == NP - 1))
                m.then_inc(conv_done, 1)

            def transpose_conv(i, r):
                if r == 0:
                    pe.wait_ge(conv_lo, (i + 1) * C2)
                for j in range(N2):
                    if r and j % WB == 0:
                        pe.wait_ge(xcs_ready, i * R2 + 2 * (r - 1) + j // WB + 1)
                    for u in range(2):
                        m = nc.tensor.matmul(ps[:, OB + j // WB, (j % WB) * P:(j % WB + 1) * P],
                                             V[:, u, r * N2 + j], eighth[:], start=(u == 0), stop=(u == 1))
                    if j % WB == WB - 1:
                        m.then_inc(ct_done, 1)

            def project_out(i, r):
                pe.wait_ge(xc_lo, (i + 1) * R2 + 2 * (r + 1))
                for ob in range(KC):
                    if r:
                        pe.wait_ge(res_done, (i + 1) * R2 + 2 * (r - 1) + ob + 1)
                    else:
                        pe.wait_ge(v_lo, (i + 1) * R2 + ob + 1)
                    for n, (u, v) in enumerate(PASSES):
                        for e in range(2):
                            m = nc.tensor.matmul(ps[:, VB + ob, 0:ROW], wp[:, u, e, ob * P:(ob + 1) * P],
                                                 xc[:, v, r % 2, e], start=(n == 0 and e == 0),
                                                 stop=(n == NP - 1 and e == 1))
                    m.then_inc(proj_done, 1)

            project_qk(0, 0)
            project_v(0, 0)
            with pe.Fori(0, B) as i:
                for r in range(1, N1):
                    project_qk(i, r)
                    project_v(i, r)
                project_qk(i, N1)
                convolve_bank(i, 0, 0)
                convolve_bank(i, 0, 1)
                for part in range(4):
                    attend(i, N1 - 1, part)
                    if part == 1:
                        convolve_bank(i, 1, 0)
                convolve_bank(i, 1, 1)
                for s in range(2, CSTEPS):
                    for b in range(2):
                        convolve_bank(i, s, b)
                transpose_conv(i, 0)
                project_v(i, N1)
                transpose_conv(i, 1)
                scores_start(i, N1)
                for r in range(N1):
                    if 1 <= r < N1 - 1:
                        transpose_conv(i, r + 1)
                    for g in range(4 * r, min(4 * r + 4, 2 * N2)):
                        scores(i, N1, g)
                    project_out(i, r)

        @block.scalar
        def _(act):
            act.wait_ge(var_ready, 1)
            nc.scalar.activation(bna[:, 1], bna[:, 0], ACT.Sqrt).then_inc(root_ready, 1)
            act.wait_ge(weights_loaded, 16 * 3)
            nc.scalar.mul(wqk[:, 0].rearrange("p k n -> p (k n)"), w_in[:, 0:NQ], UP).then_inc(weights_hi, 1)
            nc.scalar.mul(wv[:, 0].rearrange("p k e n -> p (k e n)"), w_in[:, NQ:NQ + NV], UP).then_inc(weights_hi, 1)
            nc.scalar.mul(wp[:, 0].rearrange("p e n -> p (e n)"), w_in[:, NQ + NV:], UP_OUT).then_inc(weights_hi, 1)
            act.wait_ge(ident_ready, 1)
            nc.scalar.mul(eighth[:], ident[:], 1.0 / UP_OUT).then_inc(inits, 1)
            act.wait_ge(chain, TAPS_ZERO)
            for g in range(-(-T // WB)):
                act.wait_ge(taps_done, g + 1)
                n = min(WB, T - g * WB)
                for e in range(2):
                    m = nc.scalar.mul(
                        taps[DH * e:DH * e + T, 0, :, DH * e + g * WB:DH * e + g * WB + n],
                        ps[DH * e:DH * e + T, VB + g % 2, 0:n * P].rearrange("p (k c) -> p c k", k=n), UP)
                m.then_inc(taps_hi, 1)
            act.wait_ge(bn_ready, 1)

            def normalise(i, r):
                image = i + r // N1
                if r in (0, N1):
                    act.wait_ge(x_loaded, (image + 1) * 16)
                if r:
                    act.wait_ge(xn_lo, i * R1 + r)
                for kc in range(KC):
                    m = nc.scalar.activation(
                        xf[:, kc].rearrange("p (j a b) -> p j a b", a=WS, b=WS),
                        pixels(xb[:, image % 2, kc], r % N1), ACT.Identity,
                        bias=bna[:, 3, kc:kc + 1], scale=bna[:, 2, kc:kc + 1])
                m.then_inc(xf_ready, 1)

            def qk_high(i, r, groups):
                if r and 0 in groups:
                    act.wait_ge(s_done, i * R1 + r)
                for g in groups:
                    act.wait_ge(qk_done, i * R4 + 4 * r + g + 1)
                    nc.scalar.mul(qk[:, 0, g // 2, g % 2, 0:ROW], ps[:, QKB + g % 2, 0:ROW],
                                  1.0 / UP).then_inc(qk_hi, 1)

            def v_high(i, r):
                for b in range(2):
                    act.wait_ge(v_done, i * R2 + 2 * r + b + 1)
                    w = slice(r % N1 * N2 + WB * b, r % N1 * N2 + WB * (b + 1))
                    nc.scalar.mul(V[:, 0, w].rearrange("p w c -> p (w c)"), ps[:, VB + b], 1.0 / UP).then_inc(v_hi, 1)

            def exponentials(i, r):
                act.wait_ge(s_read, i * R1 + r + 1)
                nc.scalar.activation(Pw, Pw, ACT.Exp, scale=SCALE).then_inc(exp_ready, 1)

            def pt_high(i, r):
                for b in range(2):
                    act.wait_ge(pt_done, i * R2 + 2 * r + b + 1)
                    nc.scalar.copy(
                        PT[:, 0, 2 * b:2 * b + 2].rearrange("p r o w q -> p (r o w) q"),
                        ps[:, VB + b].rearrange("p (g q) -> p g q", q=DH)[:, :, 0:T]).then_inc(pt_hi, 1)

            def read_o(i, r):
                act.wait_ge(pv_done, i * R1 + r + 1)
                for e in range(2):
                    nc.scalar.mul(O[:, e, r], ps[:, OB + e, 0:ROW], aw[:, e:e + 1]).then_inc(o_read, 1)

            def conv_high(i, s):
                if s == 0:
                    act.wait_ge(pv_done, (i + 1) * R1)
                first = CONVB[s % 4]
                for b in range(2):
                    act.wait_ge(conv_done, i * C2 + 2 * s + b + 1)
                    cps = slice((2 * s + b) * CB, (2 * s + b + 1) * CB)
                    nc.scalar.mul(V[:, 0, :, cps], ps[:, first + b].rearrange("p (n w) -> p w n", n=CB),
                                  1.0 / UP).then_inc(conv_hi, 1)

            def xc_high(i, r):
                for b in range(2):
                    act.wait_ge(xcs_ready, i * R2 + 2 * r + b + 1)
                    t = slice(b * WB * T, (b + 1) * WB * T)
                    nc.scalar.copy(xc[:, 0, r % 2, :, t], xcs[:, :, t]).then_inc(xc_hi, 1)

            normalise(0, 0)
            qk_high(0, 0, range(4))
            normalise(0, 1)
            v_high(0, 0)
            exponentials(0, 0)
            with act.Fori(0, B) as i:
                for r in range(1, N1 + 1):
                    qk_high(i, r, (0,))
                    if r >= 2:
                        exponentials(i, r - 1)
                    qk_high(i, r, (1, 2))
                    pt_high(i, r - 1)
                    qk_high(i, r, (3,))
                    if r >= 2:
                        read_o(i, r - 2)
                    if r < N1:
                        normalise(i, r + 1)
                        v_high(i, r)
                read_o(i, N1 - 1)
                for s in range(CSTEPS):
                    conv_high(i, s)
                for r in range(N1):
                    xc_high(i, r)
                    if r == 0:
                        v_high(i, N1)
                    if r == 2:
                        normalise(i, N1 + 1)
                exponentials(i, N1)

        @block.vector
        def _(dve):
            steps = [0]

            def then(ins):
                steps[0] += 1
                ins.then_inc(chain, 1)
                dve.wait_ge(chain, steps[0])

            for u in range(2):
                then(nc.vector.memset(taps[:, u].bitcast(F32), 0.0))
            gamma, beta, mean, var = (bnp[:, n] for n in range(4))
            vare, root, scale, bias, tmp = (bna[:, n] for n in range(5))
            dve.wait_ge(loads, 16 * 6)
            nc.vector.tensor_scalar(vare, var, EPS, None, ALU.add).then_inc(var_ready, 1)
            dve.wait_ge(root_ready, 1)
            then(nc.vector.reciprocal(tmp, root))
            then(nc.vector.tensor_tensor(tmp, tmp, vare, ALU.mult))
            then(nc.vector.tensor_tensor(tmp, tmp, root, ALU.add))
            then(nc.vector.tensor_scalar(root, tmp, 0.5, None, ALU.mult))
            then(nc.vector.reciprocal(tmp, root))
            then(nc.vector.tensor_tensor(scale, gamma, tmp, ALU.mult))
            then(nc.vector.tensor_tensor(tmp, mean, scale, ALU.mult))
            nc.vector.tensor_tensor(bias, beta, tmp, ALU.subtract).then_inc(bn_ready, 1)
            for ob in range(KC):
                then(nc.vector.tensor_scalar(w7[:, ob], w7[:, ob], cw[:, 0, ob:ob + 1], None, ALU.mult))
                for n, (w, m) in enumerate(((w5, 5), (w3, 3))):
                    o = (WS - m) // 2
                    mid = w7[:, ob, o:o + m, o:o + m]
                    then(nc.vector.scalar_tensor_tensor(out=mid, in0=w[:, ob], scalar=cw[:, n + 1, ob:ob + 1],
                                                        in1=mid, op0=ALU.mult, op1=ALU.add))
                one = w7[:, ob, WS // 2, WS // 2:WS // 2 + 1]
                m = nc.vector.tensor_scalar(one, one, 1.0, None, ALU.add)
                if ob + 1 < KC:
                    then(m)
            m.then_inc(weff_ready, 1)
            dve.wait_ge(wt_done, 1)
            nc.vector.tensor_copy(weff_t.rearrange("p e o d -> p o e d"),
                                  ps[0:T, QKB, 0:C].rearrange("p (o e d) -> p o e d", o=KC, e=2)).then_inc(wt_read, 1)
            then(nc.vector.tensor_scalar(aw[:], aw[:], 1.0 / UP_OUT, None, ALU.mult))

            def low(out, whole, scale, high):
                return nc.vector.scalar_tensor_tensor(out=out, in0=whole, scalar=scale, in1=high, op0=ALU.mult,
                                                      op1=ALU.subtract)

            for n, (w, cols, up) in enumerate(((wqk, slice(0, NQ), UP), (wv, slice(NQ, NQ + NV), UP),
                                               (wp, slice(NQ + NV, NQ + NV + 2 * C), UP_OUT))):
                dve.wait_ge(weights_hi, n + 1)
                names = "abc"[:len(w.shape) - 2]
                flat = f"p {' '.join(names)} -> p ({' '.join(names)})"
                low(w[:, 1].rearrange(flat), w_in[:, cols], up, w[:, 0].rearrange(flat)).then_inc(weights_lo, 1)
            for g in range(-(-T // WB)):
                dve.wait_ge(taps_hi, g + 1)
                n = min(WB, T - g * WB)
                for e in range(2):
                    at = slice(DH * e + g * WB, DH * e + g * WB + n)
                    m = low(taps[DH * e:DH * e + T, 1, :, at],
                            ps[DH * e:DH * e + T, VB + g % 2, 0:n * P].rearrange("p (k c) -> p c k", k=n), UP,
                            taps[DH * e:DH * e + T, 0, :, at])
                m.then_inc(taps_lo, 1)
            nc.vector.memset(sm[:], 0.0).then_inc(res_done, R2)
            dve.wait_ge(inits, 4)

            def xn_high(i, r):
                if r >= 2:
                    dve.wait_ge(v_done, i * R2 + 2 * (r - 1))
                dve.wait_ge(xf_ready, i * R1 + r + 1)
                nc.vector.tensor_copy(xn[:, 0, r % 2, :, 0:ROW], xf[:]).then_inc(xn_hi, 1)

            def qk_low(i, r, groups):
                for g in groups:
                    dve.wait_ge(qk_hi, i * R4 + 4 * r + g + 1)
                    low(qk[:, 1, g // 2, g % 2, 0:ROW], ps[:, QKB + g % 2, 0:ROW], 1.0 / UP,
                        qk[:, 0, g // 2, g % 2, 0:ROW]).then_inc(qk_lo, 1)

            def v_low(i, r):
                for b in range(2):
                    dve.wait_ge(v_hi, i * R2 + 2 * r + b + 1)
                    v = V[:, :, r % N1 * N2 + WB * b:r % N1 * N2 + WB * (b + 1)].rearrange("p u w c -> p u (w c)")
                    low(v[:, 1], ps[:, VB + b], 1.0 / UP, v[:, 0]).then_inc(v_lo, 1)

            def softmax_shift(i, r):
                dve.wait_ge(s_done, i * R1 + r + 1)
                nc.vector.tensor_reduce(mx[:], S, AX_X, ALU.max).then_inc(max_ready, 1)
                dve.wait_ge(max_ready, i * R1 + r + 1)
                nc.vector.tensor_tensor(Pw, S, mx[:].unsqueeze(3).broadcast_to([P, 2, N2, T]),
                                        ALU.subtract).then_inc(s_read, 1)

            def softmax_norm(i, r):
                dve.wait_ge(exp_ready, i * R1 + r + 1)
                nc.vector.tensor_reduce(sm[:], Pw, AX_X, ALU.add).then_inc(sum_ready, 1)
                dve.wait_ge(sum_ready, i * R1 + r + 1)
                nc.vector.reciprocal(rs[:], sm[:]).then_inc(rec_ready, 1)
                dve.wait_ge(rec_ready, i * R1 + r + 1)
                nc.vector.tensor_tensor(Pw, Pw, rs[:].unsqueeze(3).broadcast_to([P, 2, N2, T]),
                                        ALU.mult).then_inc(p_ready, 1)

            def pt_low(i, r):
                for b in range(2):
                    dve.wait_ge(pt_hi, i * R2 + 2 * r + b + 1)
                    pt = PT[:, :, 2 * b:2 * b + 2].rearrange("p u r o w q -> p u (r o w) q")
                    nc.vector.tensor_tensor(pt[:, 1], ps[:, VB + b].rearrange("p (g q) -> p g q", q=DH)[:, :, 0:T],
                                            pt[:, 0], ALU.subtract).then_inc(pt_lo, 1)

            def conv_low(i, s):
                first = CONVB[s % 4]
                for b in range(2):
                    dve.wait_ge(conv_hi, i * C2 + 2 * s + b + 1)
                    cps = slice((2 * s + b) * CB, (2 * s + b + 1) * CB)
                    low(V[:, 1, :, cps], ps[:, first + b].rearrange("p (n w) -> p w n", n=CB), 1.0 / UP,
                        V[:, 0, :, cps]).then_inc(conv_lo, 1)

            def combine(i, r):
                if r == 0:
                    dve.wait_ge(o_read, (i + 1) * R2)
                for b in range(2):
                    dve.wait_ge(ct_done, i * R2 + 2 * r + b + 1)
                    dve.wait_ge(xc_lo, (i + 1) * R2 + 2 * (r - 1) + b + 1)
                    t = slice(b * WB * T, (b + 1) * WB * T)
                    nc.vector.tensor_tensor(
                        xcs[:, :, t].rearrange("p e (j q) -> p e j q", q=T),
                        ps[:, OB + b].rearrange("p (j e q) -> p e j q", j=WB, e=2)[:, :, :, 0:T],
                        O[:, :, r, t].rearrange("p e (j q) -> p e j q", q=T), ALU.add).then_inc(xcs_ready, 1)

            def residual(i, r):
                for ob in range(KC):
                    dve.wait_ge(proj_done, i * R2 + 2 * r + ob + 1)
                    px = pixels(xb[:, i % 2, ob], r)
                    nc.vector.tensor_tensor(px, ps[:, VB + ob, 0:ROW].rearrange("p (j a b) -> p j a b", a=WS, b=WS),
                                            px, ALU.add).then_inc(res_done, 1)

            xn_high(0, 0)
            qk_low(0, 0, range(4))
            xn_high(0, 1)
            v_low(0, 0)
            softmax_shift(0, 0)
            softmax_norm(0, 0)
            with dve.Fori(0, B) as i:
                for r in range(1, N1 + 1):
                    qk_low(i, r, (0,))
                    if r >= 2:
                        softmax_norm(i, r - 1)
                    qk_low(i, r, (1, 2))
                    pt_low(i, r - 1)
                    qk_low(i, r, (3,))
                    if r < N1:
                        xn_high(i, r + 1)
                        v_low(i, r)
                        softmax_shift(i, r)
                for s in range(CSTEPS):
                    conv_low(i, s)
                combine(i, 0)
                v_low(i, N1)
                for r in range(N1):
                    if r + 1 < N1:
                        combine(i, r + 1)
                    residual(i, r)
                    if r == 2:
                        xn_high(i, N1 + 1)
                    if r == 3:
                        softmax_shift(i, N1)
                softmax_norm(i, N1)


def kernel(x, L0_conv_bn_gamma, L0_conv_bn_beta, L0_conv_bn_mean, L0_conv_bn_var, L0_conv_w_qk, L0_conv_w_v,
           L0_conv_w_conv3, L0_conv_w_conv5, L0_conv_w_conv7, L0_conv_attn_w, L0_conv_c3_w, L0_conv_c5_w,
           L0_conv_c7_w, L0_conv_w_proj):
    import concourse.bacc as bacc
    import numpy as np
    from concourse.bass_utils import run_bass_kernel_spmd

    x = np.asarray(x)
    B, C, H, W = x.shape
    KC = C // P

    def halves(a):
        a = np.asarray(a)
        return np.ascontiguousarray(np.moveaxis(a.reshape(KC, P, *a.shape[1:]), 0, 1))

    w_qk, w_v, w_proj = (np.asarray(a) for a in (L0_conv_w_qk, L0_conv_w_v, L0_conv_w_proj))
    arrays = {
        "x": x.reshape(B, C, H * W),
        "w_qk_t": np.ascontiguousarray(w_qk.T.reshape(KC, P, 2 * C).transpose(1, 0, 2)).reshape(P, KC * 2 * C),
        "w_v_t": np.ascontiguousarray(w_v.T.reshape(KC, P, KC, 2, DH).transpose(1, 0, 3, 2, 4)).reshape(P, KC * C),
        "w_proj_t": np.ascontiguousarray(w_proj.T.reshape(KC, 2, DH, C).transpose(0, 2, 1, 3)).reshape(P, 2 * C),
        "bn": np.ascontiguousarray(np.stack([halves(a) for a in (L0_conv_bn_gamma, L0_conv_bn_beta, L0_conv_bn_mean,
                                                                 L0_conv_bn_var)], axis=1)),
        "attn_w": np.ascontiguousarray(np.asarray(L0_conv_attn_w).reshape(KC, 2, DH).transpose(0, 2, 1)).reshape(P, 2),
        "conv7": halves(np.asarray(L0_conv_w_conv7)[:, 0]),
        "conv5": halves(np.asarray(L0_conv_w_conv5)[:, 0]),
        "conv3": halves(np.asarray(L0_conv_w_conv3)[:, 0]),
        "conv_w": np.ascontiguousarray(np.stack([halves(np.asarray(a).reshape(C)) for a in
                                                 (L0_conv_c7_w, L0_conv_c5_w, L0_conv_c3_w)], axis=1)),
    }
    nc = bacc.Bacc("TRN2", target_bir_lowering=False, num_devices=1)
    args = [nc.dram_tensor(f"in_{n}", a.shape, mybir.dt.from_np(a.dtype), kind="ExternalInput").ap()
            for n, a in arrays.items()]
    out = nc.dram_tensor("out_x", (B, C, H * W), F32, kind="ExternalOutput").ap()
    window_attention_block(nc, *args, out)
    r = run_bass_kernel_spmd(nc, [{f"in_{n}": a for n, a in arrays.items()}], core_ids=[0])
    return r.results[0]["out_x"].reshape(B, C, H, W)
```

```python
from contextlib import ExitStack

import concourse.bass as bass
from concourse import mybir

ALU = mybir.AluOpType
ACT = mybir.ActivationFunctionType
F32 = mybir.dt.float32
F16 = mybir.dt.float16
AX_X = mybir.AxisListType.X

P = 128
WS = 7
T = WS * WS
DH = 64
EPS = 1e-5


def window_attention_block(nc, x, w_qk_t, w_v_t, w_proj_t, bn, attn_w, conv7, conv5, conv3, conv_w, out):
    B, C, HW = x.shape
    H = W = 56
    N1, N2 = H // WS, W // WS
    KC = C // P
    ROW = N2 * T
    PAD = ROW + DH - T
    PAIRS = N2 // 2
    CP = P
    T2 = 2 * T
    TS = P - DH + T + 1
    BANK = 512
    WB = BANK // P
    NW = N1 * N2
    CB = BANK // NW
    CSTEPS = CP // (2 * CB)
    SCALE = float(DH) ** -0.5
    G2 = 13
    UP = 64.0
    UP_OUT = 8.0
    PASSES = ((0, 0), (0, 1), (1, 0))
    NP = len(PASSES)

    ctx = ExitStack()
    with ctx:
        def sb(name, shape, dt=F32):
            return ctx.enter_context(nc.sbuf_tensor(name, shape, dt))

        def sem(name):
            return ctx.enter_context(nc.semaphore(name))

        ps = ctx.enter_context(nc.psum_tensor("ps", [P, 8, BANK], F32))
        QKB, VB, SB, OB = 0, 2, 4, 6

        QK_ORDER = (0, 2, 3, 1)
        CONVB = (SB, QKB, VB, OB)
        CTB = (OB, QKB)

        xb = sb("xb", [P, 2, KC, HW])
        xf = sb("xf", [P, KC, ROW])
        xn = sb("xn", [P, 2, 2, KC, PAD], F16)
        q = sb("q", [P, 2, KC, PAD], F16)
        kd = sb("kd", [P, 2, KC, N2, 2, T], F16)
        V = sb("V", [P, 2, NW, CP], F16)
        O = sb("O", [P, 2, N1, ROW])
        taps = sb("taps", [P, 2 * CP * TS + P - TS], F16)
        Pn = sb("Pn", [P, PAIRS, KC, 2, DH])
        PT = sb("PT", [P, 2, PAIRS, KC, 2, 2, T], F16)
        xc = sb("xc", [P, 2, 2, 2, ROW], F16)
        mx = sb("mx", [P, 2, N2])
        sm = sb("sm", [P, 2, N2])
        rs = sb("rs", [P, 2, N2])
        wqk = sb("wqk", [P, 2, KC, 2 * C], F16)
        wv = sb("wv", [P, 2, KC, 2, CP], F16)
        wp = sb("wp", [P, 2, 2, C], F16)
        ident = sb("ident", [P, P])
        eighth = sb("eighth", [P, P], F16)
        bnp = sb("bnp", [P, 4, KC])
        bna = sb("bna", [P, 5, KC])
        aw = sb("aw", [P, 2])
        ones = sb("ones", [P, 1])
        cw = sb("cw", [P, 3, KC])
        stage, used = O[:].rearrange("p e r t -> p (e r t)"), [0]

        def staged(n, parts=P):
            used[0] += n
            return stage[0:parts, used[0] - n:used[0]]

        w_in = staged(KC * 2 * C + KC * 2 * CP + 2 * C)
        w7 = staged(KC * T).rearrange("p (o a b) -> p o a b", a=WS, b=WS)
        w5 = staged(KC * 25).rearrange("p (o a b) -> p o a b", a=5, b=5)
        w3 = staged(KC * 9).rearrange("p (o a b) -> p o a b", a=3, b=3)
        weff_t = staged(C, T).rearrange("p (e o d) -> p e o d", e=2, o=KC)
        shift = staged(WS * G2 * WS, T).rearrange("p (c a b) -> p c a b", a=G2, b=WS)
        NQ, NV = KC * 2 * C, KC * 2 * CP

        loads = sem("const_loads")
        weights_loaded = sem("weights_loaded")
        inits = sem("inits")
        pool_chain = sem("pool_chain")
        ident_ready = sem("ident_ready")
        chain = sem("dve_chain")
        var_ready = sem("var_ready")
        root_ready = sem("root_ready")
        bn_ready = sem("bn_ready")
        weff_ready = sem("weff_ready")
        taps_zero = sem("taps_cleared")
        wt_done = sem("weff_transposed")
        wt_read = sem("weff_t_ready")
        taps_done = sem("taps_in_psum")
        taps_hi = sem("taps_hi")
        taps_lo = sem("taps_lo")
        weights_hi = sem("weights_hi")
        weights_lo = sem("weights_lo")
        x_loaded = sem("x_loaded")
        stored = sem("stored")
        xf_ready = sem("xf_ready")
        xn_hi = sem("xn_hi")
        xn_lo = sem("xn_lo")
        qk_done = sem("qk_done")
        qk_hi = sem("qk_hi")
        qk_lo = sem("qk_lo")
        v_done = sem("v_done")
        v_hi = sem("v_hi")
        v_lo = sem("v_lo")
        s_done = sem("s_done")
        max_ready = sem("max_ready")
        s_read = sem("s_read")
        exp_ready = sem("exp_ready")
        sum_ready = sem("sum_ready")
        rec_ready = sem("rec_ready")
        p_ready = sem("p_ready")
        pt_done = sem("pt_done")
        pt_hi = sem("pt_hi")
        pt_lo = sem("pt_lo")
        pv_done = sem("pv_done")
        o_read = sem("o_read")
        conv_done = sem("conv_done")
        conv_hi = sem("conv_hi")
        conv_lo = sem("conv_lo")
        ct_done = sem("ct_done")
        xcs_ready = sem("xcs_ready")
        xc_hi = sem("xc_hi")
        xc_lo = sem("xc_lo")
        proj_done = sem("proj_done")
        res_done = sem("res_done")

        R1, R2, R4 = N1, 2 * N1, 4 * N1
        C2 = 2 * CSTEPS

        x_v = x.rearrange("b (k p) n -> b p k n", p=P)
        out_v = out.rearrange("b (k p) n -> b p k n", p=P)

        def pixels(t, r):
            v = t.rearrange("p (a i b j) -> p i j a b", a=WS, i=N1, b=WS, j=N2)
            return v[:, r]

        Pw = Pn[:, :, :, :, 0:T].rearrange("p (b r) o e k -> p b (r o e) k", b=2)
        S = ps[:, SB:SB + 2, 0:ROW].rearrange("p b (g k) -> p b g k", k=T)
        taps_f32 = taps[:].bitcast(F32)
        taps_half = (2 * CP * TS + P - TS) // 4
        tap_cols = taps[:, 0:2 * CP * TS].rearrange("p (u c k) -> p u c k", u=2, c=CP)

        def qk_parts(u, g):
            src = ps[:, QKB + g % 2, 0:ROW]
            h = QK_ORDER[g]
            if h < KC:
                return [(q[:, u, h, 0:ROW], src)]
            halves = [slice(DH * e, DH * (e + 1)) for e in range(2)]
            return [(kd[p, u, h - KC, :, e], src[p].rearrange("p (j t) -> p j t", t=T)) for e, p in enumerate(halves)]

        def pt_part(u, b, e):
            return PT[DH * e:DH * (e + 1), u, 2 * b:2 * b + 2, :, :, e].rearrange("p r o w q -> p (r o w) q")

        def pt_source(b, e):
            return ps[DH * e:DH * (e + 1), VB + b].rearrange("p (g q) -> p g q", q=DH)[:, :, 0:T]


        block = ctx.enter_context(nc.Block())

        @block.sync
        def _(sp):
            def load(n, buf):
                sp.dma_start(xb[:, buf], x_v[n]).then_inc(x_loaded, 16)

            def store(n, buf):
                sp.dma_start(out_v[n], xb[:, buf]).then_inc(stored, 16)

            for dst, src in ((bnp[:], bn), (w7, conv7), (w5, conv5), (w3, conv3), (cw[:], conv_w),
                             (aw[:], attn_w)):
                sp.dma_start(dst, src).then_inc(loads, 16)
            load(0, 0)
            for dst, src in ((w_in[:, 0:NQ], w_qk_t), (w_in[:, NQ:NQ + NV], w_v_t), (w_in[:, NQ + NV:], w_proj_t)):
                sp.dma_start(dst, src).then_inc(weights_loaded, 16)
            sp.wait_ge(x_loaded, 16)
            load(1, 1)
            with sp.Fori(0, B - 2) as i:
                sp.wait_ge(res_done, (i + 2) * R2)
                store(i, i % 2)
                sp.wait_ge(stored, (i + 1) * 16)
                sp.wait_ge(x_loaded, (i + 2) * 16)
                load(i + 2, i % 2)
            for i in range(B - 2, B):
                sp.wait_ge(res_done, (i + 2) * R2)
                store(i, i % 2)
                if i == B - 2:
                    sp.wait_ge(x_loaded, B * 16)
                    sp.sem_inc(x_loaded, 16)
            sp.wait_ge(stored, B * 16)

        @block.gpsimd
        def _(pool):
            nc.gpsimd.memset(ident[:], 0.0).then_inc(pool_chain, 1)
            nc.gpsimd.memset(shift, 0.0).then_inc(pool_chain, 1)
            nc.gpsimd.memset(ones[:], 1.0).then_inc(pool_chain, 1)
            pool.wait_ge(pool_chain, 3)
            nc.gpsimd.affine_select(out=ident[:], in_=ident[:], compare_op=ALU.not_equal, fill=1.0, base=0,
                                    pattern=[[-1, P]], channel_multiplier=1).then_inc(ident_ready, 1)
            R = WS // 2
            for b_out in range(WS):
                lo, hi = max(0, b_out - R), min(WS, b_out + R + 1)
                mid = shift[:, b_out, R:R + WS, lo:hi]
                m = nc.gpsimd.affine_select(out=mid, in_=mid, compare_op=ALU.not_equal, fill=1.0,
                                            base=-(lo - b_out + R), pattern=[[-WS, WS], [-1, hi - lo]],
                                            channel_multiplier=1)
            m.then_inc(ident_ready, 1)
            nc.gpsimd.memset(taps_f32[:, taps_half:], 0.0).then_inc(taps_zero, 1)
            for t in (xn, q, kd, Pn, PT):
                nc.gpsimd.memset(t[:], 0.0).then_inc(inits, 1)

            pool.wait_ge(inits, 6)

            def split_xn(i, r):
                if r >= 2:
                    pool.wait_ge(v_done, i * R2 + 2 * (r - 1))
                pool.wait_ge(xf_ready, i * R1 + r + 1)
                nc.gpsimd.tensor_tensor(xn[:, 0, r % 2, :, 0:ROW], xf[:],
                                        ones[:].unsqueeze(2).broadcast_to([P, KC, ROW]), ALU.mult).then_inc(xn_hi, 1)
                pool.wait_ge(xn_hi, i * R1 + r + 1)
                nc.gpsimd.tensor_tensor(xn[:, 1, r % 2, :, 0:ROW], xf[:], xn[:, 0, r % 2, :, 0:ROW],
                                        ALU.subtract).then_inc(xn_lo, 1)

            def xc_low(i, r):
                for b in range(2):
                    t = slice(b * WB * T, (b + 1) * WB * T)
                    pool.wait_ge(xc_hi, i * R2 + 2 * r + b + 1)
                    nc.gpsimd.tensor_tensor(xc[:, 1, r % 2, :, t], O[:, :, r, t], xc[:, 0, r % 2, :, t],
                                            ALU.subtract).then_inc(xc_lo, 1)

            split_xn(0, 0)
            split_xn(0, 1)
            with pool.Fori(0, B) as i:
                for r in range(2, N1 + 2):
                    split_xn(i, r)
                for r in range(N1):
                    xc_low(i, r)

        @block.tensor
        def _(pe):
            pe.wait_ge(ident_ready, 2)
            pe.wait_ge(weff_ready, 1)
            for ob in range(KC):
                m = nc.tensor.transpose(ps[0:T, QKB, ob * P:(ob + 1) * P], w7[:, ob].rearrange("p a b -> p (a b)"),
                                        ident[:])
            m.then_inc(wt_done, 1)
            pe.wait_ge(wt_read, 1)
            for k in range(T):
                a, b = k // WS, k % WS
                if k % WB == 0 and k >= 2 * WB:
                    pe.wait_ge(taps_lo, k // WB - 1)
                for e in range(2):
                    m = nc.tensor.matmul(ps[DH * e:DH * e + T, VB + (k // WB) % 2, (k % WB) * P:(k % WB + 1) * P],
                                         shift[:, b, WS - 1 - a:2 * WS - 1 - a].rearrange("p a b -> p (a b)"),
                                         weff_t[:, e].rearrange("p o d -> p (o d)"), start=True, stop=True)
                if k % WB == WB - 1 or k == T - 1:
                    m.then_inc(taps_done, 1)
            pe.wait_ge(taps_lo, -(-T // WB))
            pe.wait_ge(weights_lo, 3)
            pe.wait_ge(inits, 6)

            def project_qk(i, r):
                pe.wait_ge(xn_lo, i * R1 + r + 1)
                for g in range(4):
                    if r or g >= 2:
                        pe.wait_ge(qk_lo, i * R4 + 4 * r + g - 1)
                    h = QK_ORDER[g]
                    for n, (u, v) in enumerate(PASSES):
                        for kc in range(KC):
                            m = nc.tensor.matmul(ps[:, QKB + g % 2, 0:ROW], wqk[:, u, kc, h * P:(h + 1) * P],
                                                 xn[:, v, r % 2, kc, 0:ROW], start=(n == 0 and kc == 0),
                                                 stop=(n == NP - 1 and kc == KC - 1))
                    m.then_inc(qk_done, 1)
                    if r >= 2 and g in (0, 2):
                        attend(i, r - 2, g)
                        attend(i, r - 2, g + 1)
                    if r and g in (1, 2):
                        transpose_p(i, r - 1, g - 1)

            def project_v(i, r, banks=range(2)):
                for b in banks:
                    if r == N1:
                        pe.wait_ge(conv_lo, i * C2 + 2 * (CSTEPS - 2) + b + 1)
                    elif r:
                        pe.wait_ge(pt_lo, i * R2 + 2 * (r - 1) + b + 1)
                    for j in range(WB * b, WB * (b + 1)):
                        for n, (u, v) in enumerate(PASSES):
                            for kc in range(KC):
                                for e in range(2):
                                    m = nc.tensor.matmul(
                                        ps[DH * e:DH * (e + 1), VB + b, (j % WB) * P:(j % WB + 1) * P],
                                        xn[:, u, r % 2, kc, j * T:j * T + DH], wv[:, v, kc, e],
                                        start=(n == 0 and kc == 0), stop=(n == NP - 1 and kc == KC - 1))
                        if j % WB == WB - 1:
                            m.then_inc(v_done, 1)
                        if j == 2 and r < N1:
                            scores_start(i, r)
                        if j >= 2 and r < N1:
                            for g in range(*SCORE_TURNS[j - 2]):
                                scores(i, r, g)

            SCORE_TURNS = ((0, 4), (4, 8), (8, 11), (11, 14), (14, 16), (16, 16))

            def scores_start(i, r):
                pe.wait_ge(qk_lo, i * R4 + 4 * (r + 1))

            def scores(i, r, g):
                p, ob, w = g // 4, g // 2 % 2, g % 2
                t = (2 * p + w) * T
                b, s = p // 2, (p % 2 * KC + ob) * T2
                if r and g % N2 == 0:
                    pe.wait_ge(s_read, i * R2 + 2 * (r - 1) + b + 1)
                for n, (u, v) in enumerate(PASSES):
                    m = nc.tensor.matmul(ps[DH * w:DH * (w + 1), SB + b, s:s + T2], q[:, u, ob, t:t + DH],
                                         kd[:, v, ob, 2 * p + w], start=(n == 0), stop=(n == NP - 1))
                if g % N2 == N2 - 1:
                    m.then_inc(s_done, 1)

            def transpose_p(i, r, b):
                pe.wait_ge(p_ready, i * R2 + 2 * r + b + 1)
                if r:
                    pe.wait_ge(v_lo, i * R2 + 2 * r + b + 1)
                else:
                    pe.wait_ge(res_done, i * R2 + R2)
                for p in range(2 * b, 2 * b + 2):
                    for ob in range(KC):
                        s = ((p % 2) * KC + ob) * P
                        m = nc.tensor.transpose(ps[:, VB + b, s:s + P],
                                                Pn[:, p, ob].rearrange("p e k -> p (e k)"), ident[:])
                m.then_inc(pt_done, 1)

            def attend(i, r, part):
                if part == 0:
                    pe.wait_ge(pt_lo, i * R2 + 2 * (r + 1))
                    if r:
                        pe.wait_ge(o_read, i * R2 + 2 * r)
                for j in range(2 * part, 2 * part + 2):
                    for n, (u, v) in enumerate(PASSES):
                        for ob in range(KC):
                            m = nc.tensor.matmul(
                                ps[DH * ob:DH * (ob + 1), OB + j // WB, j % WB * T2:(j % WB + 1) * T2],
                                V[:, u, r * N2 + j, ob * DH:(ob + 1) * DH], PT[:, v, j // 2, ob, j % 2],
                                start=(n == 0), stop=(n == NP - 1))
                if part == 3:
                    m.then_inc(pv_done, 1)

            def convolve_bank(i, s, b):
                first = CONVB[s % 4]
                if s == 0 and b == 0:
                    pe.wait_ge(v_lo, (i + 1) * R2)
                if s == 0:
                    pe.wait_ge(s_read, (i + 1) * R2)
                elif s == 1:
                    pe.wait_ge(qk_lo, (i + 1) * R4 + 4)
                elif s == 2:
                    pe.wait_ge(pt_lo, (i + 1) * R2)
                elif s == 3:
                    pe.wait_ge(o_read, (i + 1) * R2)
                else:
                    pe.wait_ge(conv_lo, i * C2 + 2 * (s - 4) + b + 1)
                for n8 in range(CB):
                    cp = (2 * s + b) * CB + n8
                    for n, (u, v) in enumerate(PASSES):
                        at = (u * CP + cp) * TS
                        m = nc.tensor.matmul(ps[:, first + b, n8 * NW:(n8 + 1) * NW], taps[:, at:at + P],
                                             V[:, v, :, cp], start=(n == 0), stop=(n == NP - 1))
                m.then_inc(conv_done, 1)

            def transpose_conv(i, r):
                if r == 0:
                    pe.wait_ge(conv_lo, (i + 1) * C2)
                for j in range(N2):
                    if r >= 2 and j % WB == 0:
                        pe.wait_ge(xcs_ready, i * R2 + 2 * (r - 2) + j // WB + 1)
                    for u in range(2):
                        m = nc.tensor.matmul(ps[:, CTB[r % 2] + j // WB, j % WB * P:j % WB * P + DH + T],
                                             V[:, u, r * N2 + j], eighth[:, 0:DH + T], start=(u == 0), stop=(u == 1))
                    if j % WB == WB - 1:
                        m.then_inc(ct_done, 1)

            def project_out(i, r):
                pe.wait_ge(xc_lo, i * R2 + 2 * (r + 1))
                for ob in range(KC):
                    if r:
                        pe.wait_ge(res_done, (i + 1) * R2 + 2 * (r - 1) + ob + 1)
                    else:
                        pe.wait_ge(v_lo, (i + 1) * R2 + ob + 1)
                    for n, (u, v) in enumerate(PASSES):
                        for e in range(2):
                            m = nc.tensor.matmul(ps[:, VB + ob, 0:ROW], wp[:, u, e, ob * P:(ob + 1) * P],
                                                 xc[:, v, r % 2, e], start=(n == 0 and e == 0),
                                                 stop=(n == NP - 1 and e == 1))
                    m.then_inc(proj_done, 1)

            project_qk(0, 0)
            project_v(0, 0)
            with pe.Fori(0, B) as i:
                for r in range(1, N1):
                    project_qk(i, r)
                    project_v(i, r)
                project_qk(i, N1)
                convolve_bank(i, 0, 0)
                convolve_bank(i, 0, 1)
                convolve_bank(i, 1, 0)
                for part in range(4):
                    attend(i, N1 - 1, part)
                convolve_bank(i, 1, 1)
                for s in range(2, CSTEPS):
                    for b in range(2):
                        convolve_bank(i, s, b)
                project_v(i, N1, (0,))
                transpose_conv(i, 0)
                project_v(i, N1, (1,))
                transpose_conv(i, 1)
                scores_start(i, N1)
                for r in range(N1):
                    if r + 2 < N1:
                        transpose_conv(i, r + 2)
                    for g in range(4 * r, min(4 * r + 4, 2 * N2)):
                        scores(i, N1, g)
                    project_out(i, r)

        @block.scalar
        def _(act):
            act.wait_ge(var_ready, 1)
            nc.scalar.activation(bna[:, 1], bna[:, 0], ACT.Sqrt).then_inc(root_ready, 1)
            act.wait_ge(weights_loaded, 16 * 3)
            nc.scalar.mul(wqk[:, 0].rearrange("p k n -> p (k n)"), w_in[:, 0:NQ], UP).then_inc(weights_hi, 1)
            nc.scalar.mul(wv[:, 0].rearrange("p k e n -> p (k e n)"), w_in[:, NQ:NQ + NV], UP).then_inc(weights_hi, 1)
            nc.scalar.mul(wp[:, 0].rearrange("p e n -> p (e n)"), w_in[:, NQ + NV:], UP_OUT).then_inc(weights_hi, 1)
            act.wait_ge(ident_ready, 1)
            nc.scalar.mul(eighth[:], ident[:], 1.0 / UP_OUT).then_inc(inits, 1)
            act.wait_ge(taps_zero, 2)
            for g in range(-(-T // WB)):
                act.wait_ge(taps_done, g + 1)
                n = min(WB, T - g * WB)
                for e in range(2):
                    m = nc.scalar.mul(
                        tap_cols[DH * e:DH * e + T, 0, :, DH * e + g * WB:DH * e + g * WB + n],
                        ps[DH * e:DH * e + T, VB + g % 2, 0:n * P].rearrange("p (k c) -> p c k", k=n), UP)
                m.then_inc(taps_hi, 1)
            act.wait_ge(bn_ready, 1)

            def normalise(i, r):
                image = i + r // N1
                if r in (0, N1):
                    act.wait_ge(x_loaded, (image + 1) * 16)
                if r:
                    act.wait_ge(xn_lo, i * R1 + r)
                for kc in range(KC):
                    m = nc.scalar.activation(
                        xf[:, kc].rearrange("p (j a b) -> p j a b", a=WS, b=WS),
                        pixels(xb[:, image % 2, kc], r % N1), ACT.Identity,
                        bias=bna[:, 3, kc:kc + 1], scale=bna[:, 2, kc:kc + 1])
                m.then_inc(xf_ready, 1)

            def qk_high(i, r, groups):
                if r and 0 in groups:
                    act.wait_ge(s_done, i * R2 + 2 * r)
                for g in groups:
                    act.wait_ge(qk_done, i * R4 + 4 * r + g + 1)
                    for out, src in qk_parts(0, g):
                        m = nc.scalar.mul(out, src, 1.0 / UP)
                    m.then_inc(qk_hi, 1)

            def v_high(i, r, banks=range(2)):
                for b in banks:
                    if r == N1 and b == 0:
                        act.wait_ge(ct_done, i * R2 + 2)
                    act.wait_ge(v_done, i * R2 + 2 * r + b + 1)
                    w = slice(r % N1 * N2 + WB * b, r % N1 * N2 + WB * (b + 1))
                    nc.scalar.mul(V[:, 0, w].rearrange("p w c -> p (w c)"), ps[:, VB + b], 1.0 / UP).then_inc(v_hi, 1)

            def exponentials(i, r, halves=range(2)):
                for b in halves:
                    act.wait_ge(s_read, i * R2 + 2 * r + b + 1)
                    nc.scalar.activation(Pw[:, b], Pw[:, b], ACT.Exp, scale=SCALE).then_inc(exp_ready, 1)

            def pt_high(i, r, banks):
                for b in banks:
                    act.wait_ge(pt_done, i * R2 + 2 * r + b + 1)
                    for e in range(2):
                        m = nc.scalar.copy(pt_part(0, b, e), pt_source(b, e))
                    m.then_inc(pt_hi, 1)

            def read_o(i, r):
                act.wait_ge(pv_done, i * R1 + r + 1)
                for e in range(2):
                    nc.scalar.mul(O[:, e, r].rearrange("p (b j q) -> p b j q", b=2, j=WB),
                                  ps[:, OB:OB + 2, 0:WB * T2].rearrange("p b (j e q) -> p e b j q", e=2, q=T)[:, e],
                                  aw[:, e:e + 1]).then_inc(o_read, 1)

            def conv_high(i, s):
                if s == 0:
                    act.wait_ge(pv_done, (i + 1) * R1)
                first = CONVB[s % 4]
                for b in range(2):
                    act.wait_ge(conv_done, i * C2 + 2 * s + b + 1)
                    cps = slice((2 * s + b) * CB, (2 * s + b + 1) * CB)
                    nc.scalar.mul(V[:, 0, :, cps], ps[:, first + b].rearrange("p (n w) -> p w n", n=CB),
                                  1.0 / UP).then_inc(conv_hi, 1)

            def xc_high(i, r):
                if r >= 2:
                    act.wait_ge(proj_done, i * R2 + 2 * (r - 1))
                for b in range(2):
                    act.wait_ge(xcs_ready, i * R2 + 2 * r + b + 1)
                    t = slice(b * WB * T, (b + 1) * WB * T)
                    nc.scalar.copy(xc[:, 0, r % 2, :, t], O[:, :, r, t]).then_inc(xc_hi, 1)

            normalise(0, 0)
            qk_high(0, 0, range(4))
            normalise(0, 1)
            v_high(0, 0)
            exponentials(0, 0)
            with act.Fori(0, B) as i:
                normalise(i, 2)
                for r in range(1, N1 + 1):
                    qk_high(i, r, (0,))
                    if r >= 2:
                        normalise(i, r + 1)
                    qk_high(i, r, (1,))
                    pt_high(i, r - 1, (0,))
                    qk_high(i, r, (2,))
                    pt_high(i, r - 1, (1,))
                    qk_high(i, r, (3,))
                    if r >= 2:
                        read_o(i, r - 2)
                    if r < N1:
                        v_high(i, r, (0,))
                        exponentials(i, r, (0,))
                        v_high(i, r, (1,))
                        exponentials(i, r, (1,))
                conv_high(i, 0)
                read_o(i, N1 - 1)
                for s in range(1, CSTEPS):
                    conv_high(i, s)
                v_high(i, N1, (0,))
                xc_high(i, 0)
                v_high(i, N1, (1,))
                for r in range(1, N1):
                    xc_high(i, r)
                    if r in (4, 7):
                        exponentials(i, N1, ((4, 7).index(r),))

        @block.vector
        def _(dve):
            steps = [0]

            def then(ins):
                steps[0] += 1
                ins.then_inc(chain, 1)
                dve.wait_ge(chain, steps[0])

            gamma, beta, mean, var = (bnp[:, n] for n in range(4))
            vare, root, scale, bias, tmp = (bna[:, n] for n in range(5))
            dve.wait_ge(loads, 16 * 6)
            nc.vector.tensor_scalar(vare, var, EPS, None, ALU.add).then_inc(var_ready, 1)
            dve.wait_ge(root_ready, 1)
            then(nc.vector.reciprocal(tmp, root))
            then(nc.vector.tensor_tensor(tmp, tmp, vare, ALU.mult))
            then(nc.vector.tensor_tensor(tmp, tmp, root, ALU.add))
            then(nc.vector.tensor_scalar(root, tmp, 0.5, None, ALU.mult))
            then(nc.vector.reciprocal(tmp, root))
            then(nc.vector.tensor_tensor(scale, gamma, tmp, ALU.mult))
            then(nc.vector.tensor_tensor(tmp, mean, scale, ALU.mult))
            nc.vector.tensor_tensor(bias, beta, tmp, ALU.subtract).then_inc(bn_ready, 1)
            for ob in range(KC):
                then(nc.vector.tensor_scalar(w7[:, ob], w7[:, ob], cw[:, 0, ob:ob + 1], None, ALU.mult))
                for n, (w, m) in enumerate(((w5, 5), (w3, 3))):
                    o = (WS - m) // 2
                    mid = w7[:, ob, o:o + m, o:o + m]
                    then(nc.vector.scalar_tensor_tensor(out=mid, in0=w[:, ob], scalar=cw[:, n + 1, ob:ob + 1],
                                                        in1=mid, op0=ALU.mult, op1=ALU.add))
                one = w7[:, ob, WS // 2, WS // 2:WS // 2 + 1]
                m = nc.vector.tensor_scalar(one, one, 1.0, None, ALU.add)
                if ob + 1 < KC:
                    then(m)
            m.then_inc(weff_ready, 1)
            dve.wait_ge(wt_done, 1)
            nc.vector.tensor_copy(weff_t.rearrange("p e o d -> p o e d"),
                                  ps[0:T, QKB, 0:C].rearrange("p (o e d) -> p o e d", o=KC, e=2)).then_inc(wt_read, 1)
            nc.vector.memset(taps_f32[:, 0:taps_half], 0.0).then_inc(taps_zero, 1)
            then(nc.vector.tensor_scalar(aw[:], aw[:], 1.0 / UP_OUT, None, ALU.mult))

            def low(out, whole, scale, high):
                return nc.vector.scalar_tensor_tensor(out=out, in0=whole, scalar=scale, in1=high, op0=ALU.mult,
                                                      op1=ALU.subtract)

            for n, (w, cols, up) in enumerate(((wqk, slice(0, NQ), UP), (wv, slice(NQ, NQ + NV), UP),
                                               (wp, slice(NQ + NV, NQ + NV + 2 * C), UP_OUT))):
                dve.wait_ge(weights_hi, n + 1)
                names = "abc"[:len(w.shape) - 2]
                flat = f"p {' '.join(names)} -> p ({' '.join(names)})"
                low(w[:, 1].rearrange(flat), w_in[:, cols], up, w[:, 0].rearrange(flat)).then_inc(weights_lo, 1)
            for g in range(-(-T // WB)):
                dve.wait_ge(taps_hi, g + 1)
                n = min(WB, T - g * WB)
                for e in range(2):
                    at = slice(DH * e + g * WB, DH * e + g * WB + n)
                    m = low(tap_cols[DH * e:DH * e + T, 1, :, at],
                            ps[DH * e:DH * e + T, VB + g % 2, 0:n * P].rearrange("p (k c) -> p c k", k=n), UP,
                            tap_cols[DH * e:DH * e + T, 0, :, at])
                m.then_inc(taps_lo, 1)
            nc.vector.memset(sm[:], 0.0).then_inc(res_done, R2)
            dve.wait_ge(inits, 6)

            def qk_low(i, r, groups):
                for g in groups:
                    dve.wait_ge(qk_hi, i * R4 + 4 * r + g + 1)
                    for (out, src), (high, _) in zip(qk_parts(1, g), qk_parts(0, g)):
                        m = low(out, src, 1.0 / UP, high)
                    m.then_inc(qk_lo, 1)

            def v_low(i, r, banks=range(2)):
                for b in banks:
                    dve.wait_ge(v_hi, i * R2 + 2 * r + b + 1)
                    v = V[:, :, r % N1 * N2 + WB * b:r % N1 * N2 + WB * (b + 1)].rearrange("p u w c -> p u (w c)")
                    low(v[:, 1], ps[:, VB + b], 1.0 / UP, v[:, 0]).then_inc(v_lo, 1)

            def softmax_shift(i, r, halves=range(2)):
                for b in halves:
                    n = i * R2 + 2 * r + b + 1
                    dve.wait_ge(s_done, n)
                    nc.vector.tensor_reduce(mx[:, b], S[:, b], AX_X, ALU.max).then_inc(max_ready, 1)
                    dve.wait_ge(max_ready, n)
                    nc.vector.tensor_tensor(Pw[:, b], S[:, b], mx[:, b].unsqueeze(2).broadcast_to([P, N2, T]),
                                            ALU.subtract).then_inc(s_read, 1)

            def softmax_norm(i, r, halves=range(2)):
                for b in halves:
                    n = i * R2 + 2 * r + b + 1
                    dve.wait_ge(exp_ready, n)
                    nc.vector.tensor_reduce(sm[:, b], Pw[:, b], AX_X, ALU.add).then_inc(sum_ready, 1)
                    dve.wait_ge(sum_ready, n)
                    nc.vector.reciprocal(rs[:, b], sm[:, b]).then_inc(rec_ready, 1)
                    dve.wait_ge(rec_ready, n)
                    nc.vector.tensor_tensor(Pw[:, b], Pw[:, b], rs[:, b].unsqueeze(2).broadcast_to([P, N2, T]),
                                            ALU.mult).then_inc(p_ready, 1)

            def pt_low(i, r, banks):
                for b in banks:
                    dve.wait_ge(pt_hi, i * R2 + 2 * r + b + 1)
                    for e in range(2):
                        m = nc.vector.tensor_tensor(pt_part(1, b, e), pt_source(b, e), pt_part(0, b, e),
                                                    ALU.subtract)
                    m.then_inc(pt_lo, 1)

            def conv_low(i, s):
                first = CONVB[s % 4]
                for b in range(2):
                    dve.wait_ge(conv_hi, i * C2 + 2 * s + b + 1)
                    cps = slice((2 * s + b) * CB, (2 * s + b + 1) * CB)
                    low(V[:, 1, :, cps], ps[:, first + b].rearrange("p (n w) -> p w n", n=CB), 1.0 / UP,
                        V[:, 0, :, cps]).then_inc(conv_lo, 1)

            def combine(i, r):
                if r == 0:
                    dve.wait_ge(o_read, (i + 1) * R2)
                for b in range(2):
                    dve.wait_ge(ct_done, i * R2 + 2 * r + b + 1)
                    t = slice(b * WB * T, (b + 1) * WB * T)
                    o = O[:, :, r, t].rearrange("p e (j q) -> p e j q", q=T)
                    nc.vector.tensor_tensor(
                        o, ps[:, CTB[r % 2] + b].rearrange("p (j e q) -> p e j q", j=WB, e=2)[:, :, :, 0:T], o,
                        ALU.add).then_inc(xcs_ready, 1)

            def residual(i, r):
                for ob in range(KC):
                    dve.wait_ge(proj_done, i * R2 + 2 * r + ob + 1)
                    px = pixels(xb[:, i % 2, ob], r)
                    nc.vector.tensor_tensor(px, ps[:, VB + ob, 0:ROW].rearrange("p (j a b) -> p j a b", a=WS, b=WS),
                                            px, ALU.add).then_inc(res_done, 1)

            qk_low(0, 0, range(4))
            v_low(0, 0)
            softmax_shift(0, 0)
            softmax_norm(0, 0, (0,))
            with dve.Fori(0, B) as i:
                for r in range(1, N1 + 1):
                    qk_low(i, r, (0,))
                    softmax_norm(i, r - 1, (1,))
                    qk_low(i, r, (1,))
                    pt_low(i, r - 1, (0,))
                    qk_low(i, r, (2, 3))
                    pt_low(i, r - 1, (1,))
                    if r < N1:
                        v_low(i, r, (0,))
                        softmax_shift(i, r)
                        softmax_norm(i, r, (0,))
                        v_low(i, r, (1,))
                for s in range(CSTEPS):
                    conv_low(i, s)
                v_low(i, N1, (0,))
                combine(i, 0)
                v_low(i, N1, (1,))
                combine(i, 1)
                for r in range(N1):
                    if r + 2 < N1:
                        combine(i, r + 2)
                    residual(i, r)
                    if r in (1, 3):
                        softmax_shift(i, N1, (r // 2,))
                    if r == N1 - 2:
                        softmax_norm(i, N1, (0,))


def kernel(x, L0_conv_bn_gamma, L0_conv_bn_beta, L0_conv_bn_mean, L0_conv_bn_var, L0_conv_w_qk, L0_conv_w_v,
           L0_conv_w_conv3, L0_conv_w_conv5, L0_conv_w_conv7, L0_conv_attn_w, L0_conv_c3_w, L0_conv_c5_w,
           L0_conv_c7_w, L0_conv_w_proj):
    import concourse.bacc as bacc
    import numpy as np
    from concourse.bass_utils import run_bass_kernel_spmd

    x = np.asarray(x)
    B, C, H, W = x.shape
    KC = C // P

    def halves(a):
        a = np.asarray(a)
        return np.ascontiguousarray(np.moveaxis(a.reshape(KC, P, *a.shape[1:]), 0, 1))

    w_qk, w_v, w_proj = (np.asarray(a) for a in (L0_conv_w_qk, L0_conv_w_v, L0_conv_w_proj))
    arrays = {
        "x": x.reshape(B, C, H * W),
        "w_qk_t": np.ascontiguousarray(w_qk.T.reshape(KC, P, 2 * C).transpose(1, 0, 2)).reshape(P, KC * 2 * C),
        "w_v_t": np.ascontiguousarray(w_v.T.reshape(KC, P, KC, 2, DH).transpose(1, 0, 3, 2, 4)).reshape(P, KC * C),
        "w_proj_t": np.ascontiguousarray(w_proj.T.reshape(KC, 2, DH, C).transpose(0, 2, 1, 3)).reshape(P, 2 * C),
        "bn": np.ascontiguousarray(np.stack([halves(a) for a in (L0_conv_bn_gamma, L0_conv_bn_beta, L0_conv_bn_mean,
                                                                 L0_conv_bn_var)], axis=1)),
        "attn_w": np.ascontiguousarray(np.asarray(L0_conv_attn_w).reshape(KC, 2, DH).transpose(0, 2, 1)).reshape(P, 2),
        "conv7": halves(np.asarray(L0_conv_w_conv7)[:, 0]),
        "conv5": halves(np.asarray(L0_conv_w_conv5)[:, 0]),
        "conv3": halves(np.asarray(L0_conv_w_conv3)[:, 0]),
        "conv_w": np.ascontiguousarray(np.stack([halves(np.asarray(a).reshape(C)) for a in
                                                 (L0_conv_c7_w, L0_conv_c5_w, L0_conv_c3_w)], axis=1)),
    }
    nc = bacc.Bacc("TRN2", target_bir_lowering=False, num_devices=1)
    args = [nc.dram_tensor(f"in_{n}", a.shape, mybir.dt.from_np(a.dtype), kind="ExternalInput").ap()
            for n, a in arrays.items()]
    out = nc.dram_tensor("out_x", (B, C, H * W), F32, kind="ExternalOutput").ap()
    window_attention_block(nc, *args, out)
    r = run_bass_kernel_spmd(nc, [{f"in_{n}": a for n, a in arrays.items()}], core_ids=[0])
    return r.results[0]["out_x"].reshape(B, C, H, W)
```
